# Optimizing a Trainium2 kernel written in Bass

```python
import numpy as np
import jax
import jax.numpy as jnp

def _softmax(x, axis=-1):
    return jax.nn.softmax(x, axis=axis)

def _gelu(x):
    return jax.nn.gelu(x, approximate=True)

def _silu(x):
    return jax.nn.silu(x)

def _sigmoid(x):
    return jax.nn.sigmoid(x)

def _layernorm(x, axis=-1, eps=1e-05):
    m = jnp.mean(x, axis=axis, keepdims=True)
    v = jnp.var(x, axis=axis, keepdims=True)
    return (x - m) / jnp.sqrt(v + eps)

def _scatter_add(tgt, idx, src, axis=0):
    return tgt.at[idx].add(src)

def _segment_sum(src, seg, n):
    return jax.ops.segment_sum(src, seg, n)
kernel_name = 'mk_sandwich_d1_jaxref_r8_f96c2a'

def setup_inputs(seed: int=0):
    np.random.seed(seed)
    _w = jnp.asarray

    def _L0_attn_setup():
        import jax, jax.numpy as jnp
        import numpy as np
        B, T, C = (2, 256, 128)
        H = 16
        D = C // H
        ROPE_BASE = 10000.0

        def _rope_tables(seq_len, dim, dtype=jnp.float32):
            inv_freq = 1.0 / ROPE_BASE ** (jnp.arange(0, dim, 2, dtype=jnp.float32) / dim)
            t = jnp.arange(seq_len, dtype=jnp.float32)
            freqs = jnp.einsum('i,j->ij', t, inv_freq)
            emb = jnp.concatenate([freqs, freqs], axis=-1)
            return (jnp.cos(emb).astype(dtype), jnp.sin(emb).astype(dtype))

        def _rotate_half(x):
            x1, x2 = jnp.split(x, 2, axis=-1)
            return jnp.concatenate([-x2, x1], axis=-1)
        key = jax.random.key(seed)
        ks = jax.random.split(key, 9)
        s = 0.02
        return {'x': jax.random.normal(ks[0], (B, T, C), jnp.float32), 'Wq': jax.random.normal(ks[1], (C, C), jnp.float32) * s, 'bq': jax.random.normal(ks[2], (C,), jnp.float32) * s, 'Wk': jax.random.normal(ks[3], (C, C), jnp.float32) * s, 'bk': jax.random.normal(ks[4], (C,), jnp.float32) * s, 'Wv': jax.random.normal(ks[5], (C, C), jnp.float32) * s, 'bv': jax.random.normal(ks[6], (C,), jnp.float32) * s, 'Wo': jax.random.normal(ks[7], (C, C), jnp.float32) * s, 'bo': jax.random.normal(ks[8], (C,), jnp.float32) * s}
    _L0_attn_in = _L0_attn_setup()

    def _L0_ffn_setup():
        import jax, jax.numpy as jnp
        import numpy as np
        D_IN, D_HID = (128, 512)

        def _ternary(key, shape):
            return jax.random.randint(key, shape, -1, 2).astype(jnp.float32)

        def _tlin(x, w, s):
            return jnp.einsum('bsi,oi->bso', x, w) * s
        key = jax.random.key(seed)
        ks = jax.random.split(key, 12)
        inv = lambda fan: 1.0 / np.sqrt(fan).astype(np.float32)
        return {'x': jax.random.normal(ks[0], (4, 256, D_IN), dtype=jnp.float32), 'w1_w': _ternary(ks[1], (D_HID, D_IN)), 'w1_s': jax.random.uniform(ks[2], (D_HID,), dtype=jnp.float32) * inv(D_IN), 'w2_w': _ternary(ks[3], (D_HID, D_IN)), 'w2_s': jax.random.uniform(ks[4], (D_HID,), dtype=jnp.float32) * inv(D_IN), 'h1_w': _ternary(ks[5], (D_HID, D_HID)), 'h1_s': jax.random.uniform(ks[6], (D_HID,), dtype=jnp.float32) * inv(D_HID), 'h2_w': _ternary(ks[7], (D_HID, D_HID)), 'h2_s': jax.random.uniform(ks[8], (D_HID,), dtype=jnp.float32) * inv(D_HID), 'w3_w': _ternary(ks[9], (D_IN, D_HID)), 'w3_s': jax.random.uniform(ks[10], (D_IN,), dtype=jnp.float32) * inv(D_HID)}
    _L0_ffn_in = _L0_ffn_setup()
    _d = {'L0_attn_x': _L0_attn_in['x'], 'L0_attn_Wq': _L0_attn_in['Wq'], 'L0_attn_bq': _L0_attn_in['bq'], 'L0_attn_Wk': _L0_attn_in['Wk'], 'L0_attn_bk': _L0_attn_in['bk'], 'L0_attn_Wv': _L0_attn_in['Wv'], 'L0_attn_bv': _L0_attn_in['bv'], 'L0_attn_Wo': _L0_attn_in['Wo'], 'L0_attn_bo': _L0_attn_in['bo'], 'L0_ffn_w1_w': _L0_ffn_in['w1_w'], 'L0_ffn_w1_s': _L0_ffn_in['w1_s'], 'L0_ffn_w2_w': _L0_ffn_in['w2_w'], 'L0_ffn_w2_s': _L0_ffn_in['w2_s'], 'L0_ffn_h1_w': _L0_ffn_in['h1_w'], 'L0_ffn_h1_s': _L0_ffn_in['h1_s'], 'L0_ffn_h2_w': _L0_ffn_in['h2_w'], 'L0_ffn_h2_s': _L0_ffn_in['h2_s'], 'L0_ffn_w3_w': _L0_ffn_in['w3_w'], 'L0_ffn_w3_s': _L0_ffn_in['w3_s']}
    _x0 = _d['L0_attn_x']
    _d['L0_attn_x'] = jax.random.normal(jax.random.fold_in(jax.random.key(seed), 1), (1, 2048, 128), dtype=_x0.dtype)
    del _x0
    return _d

def reference(L0_attn_x, L0_attn_Wq, L0_attn_bq, L0_attn_Wk, L0_attn_bk, L0_attn_Wv, L0_attn_bv, L0_attn_Wo, L0_attn_bo, L0_ffn_w1_w, L0_ffn_w1_s, L0_ffn_w2_w, L0_ffn_w2_s, L0_ffn_h1_w, L0_ffn_h1_s, L0_ffn_h2_w, L0_ffn_h2_s, L0_ffn_w3_w, L0_ffn_w3_s):

    def _L0_attn_ref(x, Wq, bq, Wk, bk, Wv, bv, Wo, bo):
        import jax, jax.numpy as jnp
        import numpy as np
        B, T, C = (2, 256, 128)
        H = 16
        D = C // H
        ROPE_BASE = 10000.0

        def _rope_tables(seq_len, dim, dtype=jnp.float32):
            inv_freq = 1.0 / ROPE_BASE ** (jnp.arange(0, dim, 2, dtype=jnp.float32) / dim)
            t = jnp.arange(seq_len, dtype=jnp.float32)
            freqs = jnp.einsum('i,j->ij', t, inv_freq)
            emb = jnp.concatenate([freqs, freqs], axis=-1)
            return (jnp.cos(emb).astype(dtype), jnp.sin(emb).astype(dtype))

        def _rotate_half(x):
            x1, x2 = jnp.split(x, 2, axis=-1)
            return jnp.concatenate([-x2, x1], axis=-1)
        b, t, c = x.shape
        q = x @ Wq.T + bq
        k = x @ Wk.T + bk
        v = x @ Wv.T + bv
        q = q.reshape(b, t, H, D).transpose(0, 2, 1, 3)
        k = k.reshape(b, t, H, D).transpose(0, 2, 1, 3)
        v = v.reshape(b, t, H, D).transpose(0, 2, 1, 3)
        cos, sin = _rope_tables(t, D, x.dtype)
        q = q * cos + _rotate_half(q) * sin
        k = k * cos + _rotate_half(k) * sin
        scale = 1.0 / jnp.sqrt(jnp.array(D, x.dtype))
        scores = jnp.einsum('bhqd,bhkd->bhqk', q, k) * scale
        causal = jnp.triu(jnp.full((t, t), -jnp.inf, dtype=x.dtype), k=1)
        scores = scores + causal
        attn = jax.nn.softmax(scores, axis=-1)
        out = jnp.einsum('bhqk,bhkd->bhqd', attn, v)
        out = out.transpose(0, 2, 1, 3).reshape(b, t, c)
        return out @ Wo.T + bo

    def _L0_ffn_ref(x, w1_w, w1_s, w2_w, w2_s, h1_w, h1_s, h2_w, h2_s, w3_w, w3_s):
        import jax, jax.numpy as jnp
        import numpy as np
        D_IN, D_HID = (128, 512)

        def _ternary(key, shape):
            return jax.random.randint(key, shape, -1, 2).astype(jnp.float32)

        def _tlin(x, w, s):
            return jnp.einsum('bsi,oi->bso', x, w) * s
        h = jax.nn.silu(_tlin(x, w1_w, w1_s)) * _tlin(x, w2_w, w2_s)
        h = jax.nn.gelu(_tlin(h, h1_w, h1_s), approximate=False)
        h = jax.nn.gelu(_tlin(h, h2_w, h2_s), approximate=False)
        return _tlin(h, w3_w, w3_s)
    x = L0_attn_x
    x = x + _layernorm(_L0_attn_ref(_layernorm(x, axis=-1), L0_attn_Wq, L0_attn_bq, L0_attn_Wk, L0_attn_bk, L0_attn_Wv, L0_attn_bv, L0_attn_Wo, L0_attn_bo), axis=-1)
    x = x + _layernorm(_L0_ffn_ref(_layernorm(x, axis=-1), L0_ffn_w1_w, L0_ffn_w1_s, L0_ffn_w2_w, L0_ffn_w2_s, L0_ffn_h1_w, L0_ffn_h1_s, L0_ffn_h2_w, L0_ffn_h2_s, L0_ffn_w3_w, L0_ffn_w3_s), axis=-1)
    return x

_drawn_inputs = setup_inputs


def setup_inputs(seed=0):
    import zlib

    import numpy as np

    out = dict(_drawn_inputs(seed))
    spreads = {}
    factors = {'L0_attn_Wq': 7.923, 'L0_attn_bq': 8.0, 'L0_attn_Wk': 7.615, 'L0_attn_bk': 8.0}
    for name, (base, spread) in spreads.items():
        noise = np.random.default_rng([zlib.crc32(name.encode()), seed]).standard_normal(out[name].shape)
        drawn = base * np.exp(spread * noise) if base else spread * noise
        out[name] = jnp.asarray(drawn.astype(out[name].dtype))
    for name, factor in factors.items():
        out[name] = (out[name] * factor).astype(out[name].dtype)
    return out
```

```python
import numpy as np

import concourse.bass as bass
from concourse import mybir
from contextlib import ExitStack

T = 2048
C = 128
H = 16
D = C // H
P = 128
HG = 4
G = H // HG
CH = 512
NC = T // CH
TPC = CH // P
F = 512
FT = F // P
PARTS = 3
KR = PARTS * PARTS * D
VW = D + 1
EPS = 1e-5
LOWEST = -3.0e38
ROPE_BASE = 10000.0
COLS = NC * HG * CH
STEPS = sum(TPC * (c + 1) for c in range(NC))
PIECES = [HG * TPC * (c + 1) for c in range(NC)]
LEAD = sum(PIECES[:NC - 1])
RING = 4
BASE = 1
PV_LAG = 2


def exp_steps(c):
    return [(c, kt, max(0, kt - TPC * c) * P) for kt in range(TPC * (c + 1))]


def max_pieces(c):
    return [(c, h, qt, kc) for h in range(HG) for qt in range(TPC) for kc in range(c + 1)]


def merged(main, side, cost_main, cost_side, by):
    out, done, at = [], 0.0, 0
    total, total_side = sum(map(cost_main, main)) * by, sum(map(cost_side, side))
    spent = 0.0
    for m in main:
        out.append(m)
        done += cost_main(m)
        while at < len(side) and spent < total_side * done / total - 1e-9:
            spent += cost_side(side[at])
            out.append(side[at])
            at += 1
    return out + side[at:]


def with_negs(side, turn_lag):
    out, due = [], []
    for n, item in enumerate(side):
        out.append(item)
        due = [(k - 1, c) for k, c in due]
        while due and due[0][0] <= 0:
            out.append(("neg_turn", due.pop(0)[1]))
        if n + 1 == len(side) or side[n + 1][1] != item[1]:
            out.append(("neg_split", item[1]))
            due.append((turn_lag, item[1]))
    return out + [("neg_turn", c) for _, c in due]


def group_plan(last):
    def exp_list(chunks):
        steps = [("exp",) + s for c in chunks for s in exp_steps(c)]
        return steps

    def cost(item):
        return {"exp": 4.0 - item[3] / P if item[0] == "exp" else 0, "max": 0}.get(item[0], 0)

    def cost_side(item):
        if item[0] != "max":
            return 0.0
        return 4.0 if item[4] < item[1] else item[3] + 1.5

    side_a = with_negs([("max",) + m for m in max_pieces(NC - 1)], 3)
    side_b = [] if last else with_negs([("max",) + m for c in range(NC - 1) for m in max_pieces(c)], 3)
    plan = merged(exp_list(range(NC - 1)), side_a, cost, cost_side, 0.85)
    plan += merged(exp_list([NC - 1]), side_b, cost, cost_side, 1.0)
    out, waiting, turns = [], [], []

    def values(step):
        out.append(("pv",) + step)
        if step[1] == TPC * (step[0] + 1) - 1:
            out.append(("o_copy", step[0]))
            turns.append([2, step[0]])

    for item in plan:
        out.append(item)
        if item[0] == "exp":
            for t in turns:
                t[0] -= 1
            while turns and turns[0][0] <= 0:
                out.append(("o_turn", turns.pop(0)[1]))
            waiting.append(item[1:])
            if len(waiting) > PV_LAG:
                values(waiting.pop(0))
    for step in waiting:
        values(step)
    out += [("o_turn", c) for _, c in turns]
    if last:
        plan, out = out, []
        due = []
        for item in plan:
            out.append(item)
            if item[0] == "exp":
                due = [[n - 1, x] for n, x in due]
                while due and due[0][0] <= 0:
                    out.append(due.pop(0)[1])
            if item[0] == "o_turn":
                c = item[1]
                due += [[2, ("a_turn", c)], [3, ("a_proj", c)], [6, ("x_turn", c)]]
                due.sort(key=lambda d: d[0])
        out += [x for _, x in due]
    return out


BODY, LAST = group_plan(False), group_plan(True)


def attention_mlp_kernel(nc, x_in, wqkv_in, bqkv_in, wo_in, bo_in, w12_in, h1_in, h2_in, w3_in,
                         scales_in, s3_in, ident_in, mask_in, rope_in, ones_in, out_dram):
    f32, bf16 = mybir.dt.float32, mybir.dt.bfloat16
    ALU, ACT, AX = mybir.AluOpType, mybir.ActivationFunctionType, mybir.AxisListType

    parts_dram = nc.dram_tensor("parts_dram", [2, NC, PARTS, D, H * CH], bf16, kind="Internal").ap()

    ctx = ExitStack()
    with ctx:
        def sb(name, shape, dt=f32):
            return ctx.enter_context(nc.sbuf_tensor(name, shape, dt))

        def sem(name):
            return ctx.enter_context(nc.semaphore(name))

        QA = sb("QA", [P, COLS], bf16)
        KM = sb("KM", [P, COLS], bf16)
        KE = sb("KE", [P, COLS], bf16)
        PR = sb("PR", [P, RING, HG, CH])
        VA = sb("VA", [P, G, T // P, HG, VW])
        VG = sb("VG", [P, T // P, HG, VW])
        X = sb("X", [P, T // P, C])
        AT = sb("AT", [P, T // P, C])
        OT = sb("OT", [P, CH])
        work = sb("work", [P, 5632])
        XN = sb("XN", [P, TPC, C])
        XT = sb("XT", [P, CH])
        pieces3 = sb("pieces3", [P, TPC, PARTS, 2 * C], bf16)
        piecesT = sb("piecesT", [P, 2 * PARTS, CH], bf16)
        wqkv = sb("wqkv", [P, 3 * C])
        bqkv = sb("bqkv", [P, 3 * C])
        wo = sb("wo", [P, C])
        bo = sb("bo", [P, C])
        s3 = sb("s3", [P, C])
        scales = sb("scales", [P, 4, FT])
        ident = sb("ident", [P, P])
        identb = sb("identb", [P, P], bf16)
        mask = sb("mask", [P, CH])
        rope = sb("rope", [P, T // P, 2, 2, D // 2])
        junk = sb("junk", [P, 4, CH], bf16)
        mpart = sb("mpart", [P, HG * TPC, NC])
        mx = sb("mx", [P, HG * TPC])
        mres = sb("mres", [P, HG * TPC])
        mneg = sb("mneg", [P, P], bf16)
        mT = sb("mT", [P, NC, P], bf16)
        rec = sb("rec", [P, TPC * HG])
        stats = sb("stats", [P, TPC, 6])
        mv = sb("mv", [P, TPC, 2])
        var = sb("var", [P, TPC])
        rstd = sb("rstd", [P, TPC])
        nhalf = sb("nhalf", [P, TPC])
        yb = sb("yb", [P, TPC, C])
        yn = sb("yn", [P, TPC, C])
        ob = sb("ob", [P, TPC, C])
        silu = sb("silu", [P, 2, CH])
        aT = sb("aT", [P, CH])
        X2T = sb("X2T", [P, T])

        def tile2(at):
            return work[:, at:at + TPC * 2 * C].rearrange("p (j n) -> p j n", j=TPC)

        qk, ra, rb, qr, qres = (tile2(n * TPC * 2 * C) for n in range(5))
        w12 = work[:, 0:2 * F].rearrange("p (a n) -> p a n", a=2)
        h1 = work[:, 2 * F:2 * F + FT * F].rearrange("p (k n) -> p k n", k=FT)
        h2 = work[:, 2 * F + FT * F:2 * F + 2 * FT * F].rearrange("p (k n) -> p k n", k=FT)
        w3 = work[:, 2 * F + 2 * FT * F:].rearrange("p (k n) -> p k n", k=FT)
        hA, hB, hC = PR[:, 0], PR[:, 1], PR[:, 2]

        PS = ctx.enter_context(nc.psum_tensor("PS", [P, 8, CH], f32))
        MAXB, OB, MISC = 4, 6, 7

        x_loaded, w_loaded, c_loaded = sem("x_loaded"), sem("w_loaded"), sem("c_loaded")
        idb_ready = sem("idb_ready")
        var_ready, rstd_ready, xn_ready = sem("var_ready"), sem("rstd_ready"), sem("xn_ready")
        xn_turned, xt_ready, qkv_ready = sem("xn_turned"), sem("xt_ready"), sem("qkv_ready")
        qk_ready, ra_ready, qr_ready = sem("qk_ready"), sem("ra_ready"), sem("qr_ready")
        hi_ready, res_ready, mid_ready = sem("hi_ready"), sem("res_ready"), sem("mid_ready")
        lo_ready, pt_turned, pt_copied = sem("lo_ready"), sem("pt_turned"), sem("pt_copied")
        pt_stored = sem("pt_stored")
        nh_ready = sem("nh_ready")
        q_loaded = [sem(f"q_loaded{c}") for c in range(NC)]
        km_loaded = [sem(f"km_loaded{c}") for c in range(NC)]
        ke_loaded = [sem(f"ke_loaded{c}") for c in range(NC)]
        negs_loaded = [sem(f"negs_loaded{c}") for c in range(NC)]
        ones_loaded = sem("ones_loaded")
        ps_ready, ps_used = sem("piece_ready"), sem("piece_used")
        neg_ready, neg_turned, neg_rows = sem("neg_ready"), sem("neg_turned"), sem("neg_rows")
        o_clear = sem("o_clear")
        st_ready, exp_done, masked = sem("scores_ready"), sem("exp_done"), sem("masked")
        vg_ready, pv_done = sem("vg_ready"), sem("pv_done")
        o_copied, o_turned = sem("o_copied"), sem("o_turned")
        at_ready, a_turned, aT_ready = sem("at_ready"), sem("a_turned"), sem("aT_ready")
        proj_ready, proj_used = sem("proj_ready"), sem("proj_used")
        x2n_ready, x2n_turned = sem("x2n_ready"), sem("x2n_turned")
        x2t_ready = sem("x2t_ready")
        mlp_loaded = sem("mlp_loaded")
        up_ready, silu_done, up_used = sem("up_ready"), sem("silu_done"), sem("up_used")
        g1_in, g1_done, g2_in, g2_done = sem("g1_in"), sem("g1_done"), sem("g2_in"), sem("g2_done")
        y_ready, y_used, o_ready, o_stored = sem("y_ready"), sem("y_used"), sem("o_ready"), sem("o_stored")
        vstep = sem("vstep")

        alone = sem("alone")
        from_base = [xn_turned, qk_ready, pt_copied, qkv_ready, pt_turned, pt_stored, lo_ready, exp_done, pv_done, o_copied, o_turned, at_ready, y_used, g2_done, up_used, o_stored] + negs_loaded

        block = ctx.enter_context(nc.Block())

        @block.sync
        def _(sp):
            for s in from_base:
                sp.sem_inc(s, BASE)
            sp.dma_start(X[:, :, :], x_in.rearrange("(t p) f -> p t f", p=P)).then_inc(x_loaded, 16)
            sp.dma_start(ident[:, :], ident_in).then_inc(w_loaded, 16)
            sp.dma_start(wqkv[:, :], wqkv_in).then_inc(w_loaded, 16)
            sp.dma_start(bqkv[:, :], bqkv_in.broadcast_to([P, 3 * C])).then_inc(w_loaded, 16)
            sp.dma_start(rope[:, :, :, :, :].rearrange("p t a b f -> p (t a b f)"), rope_in).then_inc(w_loaded, 16)
            sp.dma_start(mask[:, :], mask_in).then_inc(c_loaded, 16)
            sp.dma_start(wo[:, :], wo_in).then_inc(c_loaded, 16)
            sp.dma_start(bo[:, :], bo_in.broadcast_to([P, C])).then_inc(c_loaded, 16)
            sp.dma_start(s3[:, :], s3_in.broadcast_to([P, C])).then_inc(c_loaded, 16)
            sp.dma_start(scales[:, :, :].rearrange("p a m -> p (a m)"), scales_in).then_inc(c_loaded, 16)
            sp.dma_start(KE[KR:KR + PARTS, :], ones_in).then_inc(ones_loaded, 16)

            def load_q(g, c):
                for a in range(PARTS):
                    q = parts_dram[0, c, a, :, bass.ds(g * HG * CH, HG * CH)]
                    sp.dma_start(QA[a * PARTS * D:(a + 1) * PARTS * D, c * HG * CH:(c + 1) * HG * CH],
                                 q.unsqueeze(0).broadcast_to([PARTS, D, HG * CH])).then_inc(q_loaded[c], 16)

            def load_k(dst, loaded, g, c):
                for a in range(PARTS):
                    k = parts_dram[1, c, :, :, bass.ds(g * HG * CH, HG * CH)]
                    sp.dma_start(dst[a * PARTS * D:(a + 1) * PARTS * D, c * HG * CH:(c + 1) * HG * CH],
                                 k).then_inc(loaded[c], 16)

            def load_negs(c, n):
                sp.wait_ge(neg_rows, n)
                rows = QA[KR:KR + PARTS, c * HG * CH:(c + 1) * HG * CH]
                sp.dma_start(rows.rearrange("p (a s) -> p a s", s=P),
                             mT[0:PARTS * HG * TPC, c, :]).then_inc(negs_loaded[c], 16)

            for c in range(NC):
                sp.wait_ge(pt_copied, TPC * (c + 1) + BASE)
                for i in range(2 * PARTS):
                    sp.dma_start(parts_dram[i // PARTS, c, i % PARTS].rearrange("d (h s) -> h d s", h=H),
                                 piecesT[:, i, :]).then_inc(pt_stored, 16)
                sp.wait_ge(pt_stored, 96 * (c + 1) + BASE)
                load_q(0, c)
                load_k(KM, km_loaded, 0, c)
                load_k(KE, ke_loaded, 0, c)
            sp.dma_start(w12[:, :, :].rearrange("p a n -> p (a n)"), w12_in).then_inc(mlp_loaded, 16)
            sp.dma_start(h1, h1_in.rearrange("(k p) n -> p k n", p=P)).then_inc(mlp_loaded, 16)
            sp.dma_start(h2, h2_in.rearrange("(k p) n -> p k n", p=P)).then_inc(mlp_loaded, 16)
            sp.dma_start(w3, w3_in.rearrange("(k p) n -> p k n", p=P)).then_inc(mlp_loaded, 16)
            for c in range(NC - 1):
                load_negs(c, c + 1)
            with sp.Fori(0, G - 1) as g:
                def scores_through(c, kt):
                    steps = sum(TPC * (a + 1) for a in range(c)) + kt + 1
                    sp.wait_ge(st_ready, 2 * (STEPS * g + steps))

                for c in range(2):
                    scores_through(c, TPC * (c + 1) - 1)
                    load_q(g + 1, c)
                load_negs(NC - 1, NC * g + NC)
                sp.wait_ge(ps_ready, LEAD + sum(PIECES) * g + PIECES[-1])
                for c in range(NC):
                    load_k(KM, km_loaded, g + 1, c)
                scores_through(2, TPC * 3 - 1)
                load_q(g + 1, 2)
                load_negs(0, NC * g + NC + 1)
                scores_through(NC - 1, TPC - 1)
                load_k(KE, ke_loaded, g + 1, 0)
                load_negs(1, NC * g + NC + 2)
                for c in (1, 2):
                    scores_through(NC - 1, TPC * (c + 1) - 1)
                    load_k(KE, ke_loaded, g + 1, c)
                load_negs(2, NC * g + NC + 3)
                scores_through(NC - 1, TPC * NC - 1)
                load_k(KE, ke_loaded, g + 1, NC - 1)
                load_q(g + 1, NC - 1)
            load_negs(NC - 1, NC * G)
            with sp.Fori(0, NC) as c:
                sp.wait_ge(o_ready, c + 1)
                sp.dma_start(out_dram[bass.ds(c * CH, CH), :].rearrange("(j p) f -> p j f", p=P),
                             ob[:, :, :]).then_inc(o_stored, 16)
            sp.wait_ge(o_stored, 16 * NC + BASE)

        @block.tensor
        def _(pe):
            pe.wait_ge(w_loaded, 64)
            pe.wait_ge(idb_ready, 1)
            with pe.Fori(0, NC) as c:
                pe.wait_ge(xn_ready, c + 1)
                for j in range(TPC):
                    last = nc.tensor.transpose(PS[:, MAXB, j * P:(j + 1) * P], XN[:, j, :], ident[:, :])
                last.then_inc(xn_turned, 1)
                pe.wait_ge(xt_ready, c + 1)
                for j in range(TPC):
                    pe.wait_ge(qk_ready, TPC * c + BASE)
                    nc.tensor.matmul(PS[:, j, 0:3 * C], XT[:, j * P:(j + 1) * P], wqkv[:, :],
                                     start=True, stop=True).then_inc(qkv_ready, 1)
                for j in range(TPC):
                    pe.wait_ge(lo_ready, TPC * c + j + 1 + BASE)
                    if j >= 2:
                        pe.wait_ge(pt_copied, TPC * c + j - 1 + BASE)
                    else:
                        pe.wait_ge(pt_copied, TPC * c + BASE)
                    bank = PS[:, OB + j % 2, :].bitcast(bf16)
                    for i in range(2 * PARTS):
                        a = i // PARTS
                        last = nc.tensor.transpose(bank[:, i * P:(i + 1) * P],
                                                   pieces3[:, j, i % PARTS, a * C:(a + 1) * C], identb[:, :])
                    last.then_inc(pt_turned, 1)

            def max_piece(g, item, n):
                _, c, h, qt, kc = item
                if (h, qt, kc) == (0, 0, 0):
                    pe.wait_ge(q_loaded[c], 48 * (g + 1))
                    pe.wait_ge(km_loaded[c], 48 * (g + 1))
                if not (isinstance(n, int) and n < 2):
                    pe.wait_ge(ps_used, n - 1)
                width = CH if kc < c else (qt + 1) * P
                b = n_bank[0] % 2
                n_bank[0] += 1
                nc.tensor.matmul(PS[:, MAXB + b, 0:width],
                                 QA[0:KR, (c * HG + h) * CH + qt * P:(c * HG + h) * CH + (qt + 1) * P],
                                 KM[0:KR, (kc * HG + h) * CH:(kc * HG + h) * CH + width],
                                 start=True, stop=True).then_inc(ps_ready, 1)

            def neg_turn(n):
                pe.wait_ge(neg_ready, n)
                for reader in readers:
                    pe.wait_ge(*reader)
                readers[:] = [(neg_rows, n)]
                nc.tensor.transpose(PS[:, MISC, :].bitcast(bf16)[:, 0:P], mneg[:, :],
                                    identb[:, :]).then_inc(neg_turned, 1)

            n_bank = [0]
            readers = []
            done, negs = 0, 0
            for item in with_negs([("max",) + m for c in range(NC - 1) for m in max_pieces(c)], 3):
                if item[0] == "max":
                    max_piece(0, item, done)
                    done += 1
                elif item[0] == "neg_turn":
                    negs += 1
                    neg_turn(negs)

            def group(g, plan, last_group):
                steps, pieces, pvs, masks, negs = 0, 0, 0, 0, 0
                readers[:] = [(neg_rows, NC - 1 + NC * g), (at_ready, NC * g + BASE)]
                for item in plan:
                    kind, c = item[0], item[1]
                    if kind == "exp":
                        _, _, kt, off = item
                        if kt == 0:
                            pe.wait_ge(negs_loaded[c], 16 * (g + 1) + BASE)
                            if c == 0:
                                pe.wait_ge(ones_loaded, 16)
                            pe.wait_ge(ke_loaded[c], 48 * (g + 1))
                        for pr in range(2):
                            n = 2 * steps + pr
                            pe.wait_ge(exp_done, 2 * STEPS * g + max(n - 1, 0) + BASE)
                            for hh in range(2):
                                h = 2 * pr + hh
                                kcol = (kt // TPC * HG + h) * CH + kt % TPC * P
                                qcol = (c * HG + h) * CH + off
                                last = nc.tensor.matmul(PS[:, 2 * pr + hh, off:CH],
                                                        KE[0:KR + PARTS, kcol:kcol + P],
                                                        QA[0:KR + PARTS, qcol:qcol + CH - off],
                                                        start=True, stop=True)
                            last.then_inc(st_ready, 1)
                        steps += 1
                    elif kind == "max":
                        max_piece(g if c == NC - 1 else g + 1, item, LEAD + sum(PIECES) * g + pieces)
                        pieces += 1
                    elif kind == "neg_turn":
                        negs += 1
                        neg_turn(NC - 1 + NC * g + negs)
                    elif kind == "pv":
                        _, _, kt, off = item
                        if kt >= TPC * c:
                            masks += 1
                            pe.wait_ge(masked, NC * TPC * g + masks)
                        else:
                            pe.wait_ge(exp_done, 2 * (STEPS * g + pvs + 1) + BASE)
                        if pvs == 0:
                            pe.wait_ge(vg_ready, g + 1)
                        if kt == 0:
                            pe.wait_ge(o_copied, NC * g + c + BASE)
                            if c == 0:
                                pe.wait_ge(o_clear, 1)
                        for h in range(HG):
                            last = nc.tensor.matmul(PS[32 * h:32 * h + VW, OB, off:CH], VG[:, kt, h, :],
                                                    PR[:, pvs % RING, h, off:CH], start=(kt == 0),
                                                    stop=(kt == TPC * (c + 1) - 1))
                        last.then_inc(pv_done, 1)
                        pvs += 1
                    elif kind == "o_turn":
                        pe.wait_ge(o_copied, NC * g + c + 1 + BASE)
                        for reader in readers:
                            pe.wait_ge(*reader)
                        readers[:] = [(at_ready, NC * g + c + 1 + BASE)]
                        for j in range(TPC):
                            last = nc.tensor.transpose(PS[:, MISC, j * P:(j + 1) * P],
                                                       OT[:, j * P:(j + 1) * P], ident[:, :])
                        last.then_inc(o_turned, 1)
                    elif kind == "a_turn":
                        pe.wait_ge(at_ready, NC * (G - 1) + c + 1 + BASE)
                        for reader in readers:
                            pe.wait_ge(*reader)
                        readers[:] = [(aT_ready, c + 1)]
                        for j in range(TPC):
                            last = nc.tensor.transpose(PS[:, MISC, j * P:(j + 1) * P],
                                                       AT[:, TPC * c + j, :], ident[:, :])
                        last.then_inc(a_turned, 1)
                    elif kind == "a_proj":
                        pe.wait_ge(aT_ready, c + 1)
                        if c == 0:
                            pe.wait_ge(c_loaded, 80)
                        for reader in readers:
                            pe.wait_ge(*reader)
                        readers[:] = [(proj_used, c + 1)]
                        for j in range(TPC):
                            last = nc.tensor.matmul(PS[:, MISC, j * P:(j + 1) * P], aT[:, j * P:(j + 1) * P],
                                                    wo[:, :], start=True, stop=True)
                        last.then_inc(proj_ready, 1)
                    elif kind == "x_turn":
                        pe.wait_ge(x2n_ready, c + 1)
                        for reader in readers:
                            pe.wait_ge(*reader)
                        readers[:] = [(x2t_ready, c + 1)]
                        for j in range(TPC):
                            last = nc.tensor.transpose(PS[:, MISC, j * P:(j + 1) * P], yn[:, j, :], ident[:, :])
                        last.then_inc(x2n_turned, 1)

            with pe.Fori(0, G - 1) as g:
                group(g, BODY, False)
            group(G - 1, LAST, True)

            pe.wait_ge(mlp_loaded, 64)
            pe.wait_ge(x2t_ready, NC)
            with pe.Fori(0, NC) as c:
                for m in range(FT):
                    if m >= 2:
                        pe.wait_ge(up_used, FT * c + m - 1 + BASE)
                    else:
                        pe.wait_ge(g2_done, FT * c + BASE)
                    for a in range(2):
                        last = nc.tensor.matmul(PS[:, 2 * (m % 2) + a, :], w12[:, a, m * P:(m + 1) * P],
                                                X2T[:, bass.ds(c * CH, CH)], start=True, stop=True)
                    last.then_inc(up_ready, 1)
                pe.wait_ge(y_used, c + BASE)
                for k in range(FT):
                    pe.wait_ge(up_used, FT * c + k + 1 + BASE)
                    for m in range(FT):
                        last = nc.tensor.matmul(PS[:, 4 + m, :], h1[:, k, m * P:(m + 1) * P], hA[:, k, :],
                                                start=(k == 0), stop=(k == FT - 1))
                        if k == FT - 1:
                            last.then_inc(g1_in, 1)
                for k in range(FT):
                    pe.wait_ge(g1_done, FT * c + k + 1)
                    for m in range(FT):
                        last = nc.tensor.matmul(PS[:, m, :], h2[:, k, m * P:(m + 1) * P], hB[:, k, :],
                                                start=(k == 0), stop=(k == FT - 1))
                        if k == FT - 1:
                            last.then_inc(g2_in, 1)
                for k in range(FT):
                    pe.wait_ge(g2_done, FT * c + k + 1 + BASE)
                    for j in range(TPC):
                        last = nc.tensor.matmul(PS[:, 4 + j, 0:C], hC[:, k, j * P:(j + 1) * P], w3[:, k, :],
                                                start=(k == 0), stop=(k == FT - 1))
                last.then_inc(y_ready, 1)

        @block.scalar
        def _(act):
            with act.Fori(0, NC) as c:
                act.wait_ge(xn_turned, c + 1 + BASE)
                act.wait_ge(qkv_ready, TPC * c + BASE)
                nc.scalar.activation(XT[:, :], PS[:, MAXB, :], ACT.Copy).then_inc(xt_ready, 1)
                act.wait_ge(pt_turned, TPC * c + BASE)
                for j in range(TPC):
                    act.wait_ge(qr_ready, TPC * c + j + 1)
                    nc.scalar.activation(pieces3[:, j, 0, :], qr[:, j, :], ACT.Copy).then_inc(hi_ready, 1)
                for j in range(TPC):
                    act.wait_ge(res_ready, TPC * c + j + 1)
                    nc.scalar.activation(pieces3[:, j, 1, :], qres[:, j, :], ACT.Copy).then_inc(mid_ready, 1)
                act.wait_ge(pt_stored, 96 * c + BASE)
                for j in range(TPC):
                    act.wait_ge(pt_turned, TPC * c + j + 1 + BASE)
                    bank = PS[:, OB + j % 2, :].bitcast(bf16)[:, 0:2 * PARTS * P]
                    nc.scalar.activation(piecesT[:, :, j * P:(j + 1) * P],
                                         bank.rearrange("p (i s) -> p i s", s=P), ACT.Copy).then_inc(pt_copied, 1)

            def group(g, plan):
                steps, pvs = 0, 0
                for item in plan:
                    kind, c = item[0], item[1]
                    if kind == "exp":
                        off = item[3]
                        act.wait_ge(pv_done, STEPS * g + max(steps - RING + 1, 0) + BASE)
                        for pr in range(2):
                            act.wait_ge(st_ready, 2 * (STEPS * g + steps) + pr + 1)
                            nc.scalar.activation(PR[:, steps % RING, 2 * pr:2 * pr + 2, off:CH],
                                                 PS[:, 2 * pr:2 * pr + 2, off:CH], ACT.Exp).then_inc(exp_done, 1)
                        steps += 1
                    elif kind == "pv":
                        pvs += 1
                    elif kind == "o_copy":
                        act.wait_ge(pv_done, STEPS * g + pvs + BASE)
                        act.wait_ge(o_turned, NC * g + c + BASE)
                        nc.scalar.activation(OT[:, :], PS[:, OB, :], ACT.Copy).then_inc(o_copied, 1)

            with act.Fori(0, G - 1) as g:
                group(g, BODY)
            group(G - 1, LAST)

            with act.Fori(0, NC) as c:
                for m in range(FT):
                    act.wait_ge(up_ready, FT * c + m + 1)
                    if m >= 2:
                        act.wait_ge(up_used, FT * c + m - 1 + BASE)
                    else:
                        act.wait_ge(up_used, FT * c + BASE)
                    nc.scalar.activation(silu[:, m % 2, :], PS[:, 2 * (m % 2), :], ACT.Silu,
                                         scale=scales[:, 0, m:m + 1]).then_inc(silu_done, 1)
                for m in range(FT):
                    act.wait_ge(g1_in, FT * c + m + 1)
                    nc.scalar.activation(hB[:, m, :], PS[:, 4 + m, :], ACT.Gelu,
                                         scale=scales[:, 2, m:m + 1]).then_inc(g1_done, 1)
                for m in range(FT):
                    act.wait_ge(g2_in, FT * c + m + 1)
                    nc.scalar.activation(hC[:, m, :], PS[:, m, :], ACT.Gelu,
                                         scale=scales[:, 3, m:m + 1]).then_inc(g2_done, 1)

        @block.gpsimd
        def _(pool):
            nc.gpsimd.memset(nhalf[:, :], -0.5).then_inc(nh_ready, 1)
            pool.wait_ge(nh_ready, 1)
            pool.wait_ge(w_loaded, 64)

            def rsqrt(n):
                pool.wait_ge(var_ready, n)
                nc.gpsimd.tensor_tensor(rstd[:, :], var[:, :], nhalf[:, :], ALU.pow).then_inc(rstd_ready, 1)

            with pool.Fori(0, NC) as c:
                rsqrt(c + 1)
                for j in range(TPC):
                    pool.wait_ge(qk_ready, TPC * c + j + 1 + BASE)
                    cos = rope[:, bass.ds(TPC * c + j, 1), 0, :, :].rearrange("p t b f -> p (t b) f")
                    nc.gpsimd.tensor_tensor(
                        ra[:, j, :].rearrange("p (b h f) -> p b h f", b=2, f=D // 2),
                        qk[:, j, :].rearrange("p (b h f) -> p b h f", b=2, f=D // 2),
                        cos.unsqueeze(2).broadcast_to([P, 2, 2 * H, D // 2]), ALU.mult).then_inc(ra_ready, 1)
                for j in range(TPC):
                    pool.wait_ge(mid_ready, TPC * c + j + 1)
                    nc.gpsimd.tensor_tensor(pieces3[:, j, 2, :], qres[:, j, :], pieces3[:, j, 1, :],
                                            ALU.subtract).then_inc(lo_ready, 1)

            def group(g, plan):
                steps, lns = 0, NC
                for item in plan:
                    kind, c = item[0], item[1]
                    if kind == "exp":
                        _, _, kt, off = item
                        if kt >= TPC * c:
                            pool.wait_ge(exp_done, 2 * (STEPS * g + steps + 1) + BASE)
                            diag = PR[:, steps % RING, :, off:off + P]
                            pool.sem_inc(alone, 1)
                            nc.gpsimd.affine_select(out=diag, in_=diag, compare_op=ALU.is_ge, fill=0.0, base=0,
                                                    pattern=[[0, HG], [1, P]],
                                                    channel_multiplier=-1).then_inc(masked, 1)
                        steps += 1
                    elif kind == "a_proj":
                        for _ in range(2):
                            lns += 1
                            rsqrt(lns)

            with pool.Fori(0, G - 1) as g:
                group(g, BODY)
            group(G - 1, LAST)
            with pool.Fori(0, NC) as c:
                rsqrt(3 * NC + c + 1)

        @block.vector
        def _(dve):
            count, base = [0], [0]

            def link(ins):
                count[0] += 1
                ins.then_inc(vstep, 1)
                dve.wait_ge(vstep, base[0] + count[0])


            def norm_stats(src, n):
                for j in range(TPC):
                    last = nc.vector.bn_stats(stats[:, j, :], src(j))
                link(last)
                dve.sem_inc(alone, 1)
                for j in range(TPC):
                    last = nc.vector.bn_aggr(mv[:, j, :], stats[:, j, :])
                link(last)
                nc.vector.tensor_scalar(var[:, :], mv[:, :, 1], EPS, None, ALU.add).then_inc(var_ready, 1)
                dve.wait_ge(rstd_ready, n)

            def normed(dst, src, j):
                return nc.vector.tensor_scalar(dst, src, mv[:, j, 0:1], rstd[:, j:j + 1],
                                               ALU.subtract, ALU.mult)

            nc.vector.memset(VA[:, :, :, :, D:VW].rearrange("p g t h v -> p (g t h) v"), 1.0)
            dve.wait_ge(w_loaded, 64)
            nc.vector.tensor_copy(identb[:, :], ident[:, :]).then_inc(idb_ready, 1)
            dve.wait_ge(x_loaded, 16)
            LINKS_P = 2 + TPC
            with dve.Fori(0, NC) as c:
                base[0], count[0] = LINKS_P * c, 0
                norm_stats(lambda j: X[:, bass.ds(TPC * c + j, 1), :].rearrange("p t f -> p (t f)"), c + 1)
                dve.wait_ge(xn_turned, c + BASE)
                for j in range(TPC):
                    last = normed(XN[:, j, :], X[:, bass.ds(TPC * c + j, 1), :].rearrange("p t f -> p (t f)"), j)
                last.then_inc(xn_ready, 1)
                for j in range(TPC):
                    dve.wait_ge(qkv_ready, TPC * c + j + 1 + BASE)
                    v = VA[:, :, bass.ds(TPC * c + j, 1), :, 0:D].rearrange("p g t h d -> p g (t h) d")
                    nc.vector.tensor_tensor(v, PS[:, j, 2 * C:3 * C].rearrange("p (g h d) -> p g h d", g=G, d=D),
                                            bqkv[:, 2 * C:3 * C].rearrange("p (g h d) -> p g h d", g=G, d=D), ALU.add)
                    nc.vector.tensor_tensor(qk[:, j, :], PS[:, j, 0:2 * C], bqkv[:, 0:2 * C],
                                            ALU.add).then_inc(qk_ready, 1)
                    dve.wait_ge(qk_ready, TPC * c + j + 1 + BASE)
                    halves = qk[:, j, :].rearrange("p (b h s f) -> p b h s f", b=2, s=2, f=D // 2)
                    turned = rb[:, j, :].rearrange("p (b h s f) -> p b h s f", b=2, s=2, f=D // 2)
                    sin = rope[:, bass.ds(TPC * c + j, 1), 1, :, :].rearrange("p t b f -> p (t b) f")
                    sin = sin.unsqueeze(2).broadcast_to([P, 2, H, D // 2])
                    nc.vector.tensor_tensor(turned[:, :, :, 0, :], halves[:, :, :, 1, :], sin, ALU.mult)
                    link(nc.vector.tensor_tensor(turned[:, :, :, 1, :], halves[:, :, :, 0, :], sin, ALU.mult))
                    dve.wait_ge(ra_ready, TPC * c + j + 1)
                    a, b, r = (t[:, j, :].rearrange("p (n s f) -> p n s f", s=2, f=D // 2) for t in (ra, rb, qr))
                    nc.vector.tensor_tensor(r[:, :, 0, :], a[:, :, 0, :], b[:, :, 0, :], ALU.subtract)
                    nc.vector.tensor_tensor(r[:, :, 1, :], a[:, :, 1, :], b[:, :, 1, :], ALU.add).then_inc(qr_ready, 1)
                dve.wait_ge(lo_ready, TPC * c + BASE)
                for j in range(TPC):
                    dve.wait_ge(hi_ready, TPC * c + j + 1)
                    nc.vector.tensor_tensor(qres[:, j, :], qr[:, j, :], pieces3[:, j, 0, :],
                                            ALU.subtract).then_inc(res_ready, 1)
                assert count[0] == LINKS_P

            nc.vector.memset(mneg[:, :], 0.0)
            dve.wait_ge(c_loaded, 80)
            dve.wait_ge(pt_copied, NC * TPC + BASE)
            nc.vector.memset(PS[:, OB, :], 0.0).then_inc(o_clear, 1)

            def max_piece(item, n):
                _, c, h, qt, kc = item
                dve.wait_ge(ps_ready, n + 1)
                if kc == c:
                    dve.sem_inc(alone, 1)
                b = n_bank[0] % 2
                n_bank[0] += 1
                row = h * TPC + qt
                if kc < c:
                    nc.vector.tensor_reduce(mpart[:, row, kc:kc + 1], PS[:, MAXB + b, :], AX.X,
                                            ALU.max).then_inc(ps_used, 1)
                else:
                    width = (qt + 1) * P
                    nc.vector.tensor_tensor_reduce(junk[:, qt, 0:width], PS[:, MAXB + b, 0:width],
                                                   mask[:, CH - width:CH], 1.0, LOWEST, ALU.add, ALU.max,
                                                   mpart[:, row, kc:kc + 1]).then_inc(ps_used, 1)

            def neg_split(c, n):
                dve.wait_ge(ps_used, n)
                hi, mid, lo = (mneg[:, a * HG * TPC:(a + 1) * HG * TPC] for a in range(PARTS))
                link(nc.vector.tensor_reduce(mx[:, :], mpart[:, :, 0:c + 1], AX.X, ALU.max))
                link(nc.vector.tensor_scalar(hi, mx[:, :], -1.0, None, ALU.mult))
                link(nc.vector.scalar_tensor_tensor(out=mres[:, :], in0=mx[:, :], scalar=-1.0, in1=hi,
                                                    op0=ALU.mult, op1=ALU.subtract))
                link(nc.vector.tensor_copy(mid, mres[:, :]))
                nc.vector.tensor_tensor(lo, mres[:, :], mid, ALU.subtract).then_inc(neg_ready, 1)

            def neg_copy(g, c, n):
                dve.wait_ge(neg_turned, n)
                dve.wait_ge(negs_loaded[c], 16 * g + BASE)
                nc.vector.tensor_copy(mT[0:PARTS * HG * TPC, c, :],
                                      PS[0:PARTS * HG * TPC, MISC, :].bitcast(bf16)[:, 0:P]).then_inc(neg_rows, 1)

            n_bank = [0]
            base[0], count[0] = LINKS_P * NC, 0
            pieces, negs = 0, 0
            for item in with_negs([("max",) + m for c in range(NC - 1) for m in max_pieces(c)], 3):
                if item[0] == "max":
                    max_piece(item, pieces)
                    pieces += 1
                elif item[0] == "neg_split":
                    neg_split(item[1], pieces)
                else:
                    negs += 1
                    neg_copy(0, item[1], negs)
            START = LINKS_P * NC + count[0]
            LINKS_G = 4 * NC + NC

            def group(g, plan, last_group):
                base[0], count[0] = START + LINKS_G * g, 0
                pieces, negs, lns = 0, 0, NC
                dve.wait_ge(pv_done, STEPS * g + BASE)
                vg = VA[:, bass.ds(g, 1), :, :, :].rearrange("p g t h v -> p (g t h v)")
                nc.vector.tensor_copy(VG[:, :, :, :].rearrange("p t h v -> p (t h v)"), vg).then_inc(vg_ready, 1)
                for item in plan:
                    kind, c = item[0], item[1]
                    if kind == "max":
                        max_piece(item, LEAD + sum(PIECES) * g + pieces)
                        pieces += 1
                    elif kind == "neg_split":
                        neg_split(c, LEAD + sum(PIECES) * g + pieces)
                    elif kind == "neg_turn":
                        negs += 1
                        neg_copy(g if c == NC - 1 else g + 1, c, NC - 1 + NC * g + negs)
                    elif kind == "o_turn":
                        dve.wait_ge(o_turned, NC * g + c + 1 + BASE)
                        o = PS[:, MISC, :].rearrange("p (j h v) -> p j h v", j=TPC, h=HG)
                        r = rec[:, :].rearrange("p (j h v) -> p j h v", j=TPC, h=HG)
                        link(nc.vector.reciprocal(r, o[:, :, :, D:VW]))
                        dst = AT[:, TPC * c:TPC * (c + 1), bass.ds(g * HG * D, HG * D)]
                        nc.vector.tensor_tensor(dst.rearrange("p j (h d) -> p j h d", d=D), o[:, :, :, 0:D],
                                                r.broadcast_to([P, TPC, HG, D]), ALU.mult).then_inc(at_ready, 1)
                    elif kind == "a_turn":
                        dve.wait_ge(a_turned, c + 1)
                        nc.vector.tensor_copy(aT[:, :], PS[:, MISC, :]).then_inc(aT_ready, 1)
                    elif kind == "a_proj":
                        dve.wait_ge(proj_ready, c + 1)
                        y = PS[:, MISC, :].rearrange("p (j f) -> p j f", j=TPC)
                        bias = bo[:, :].unsqueeze(1).broadcast_to([P, TPC, C])
                        nc.vector.tensor_tensor(yb[:, :, :], y, bias, ALU.add).then_inc(proj_used, 1)
                        dve.wait_ge(proj_used, c + 1)
                        lns += 1
                        norm_stats(lambda j: yb[:, j, :], lns)
                        dve.wait_ge(x2n_turned, c)
                        for j in range(TPC):
                            last = normed(yn[:, j, :], yb[:, j, :], j)
                        link(last)
                        xc = X[:, TPC * c:TPC * (c + 1), :]
                        link(nc.vector.tensor_tensor(xc, xc, yn[:, :, :], ALU.add))
                        lns += 1
                        norm_stats(lambda j: X[:, TPC * c + j, :], lns)
                        for j in range(TPC):
                            last = normed(yn[:, j, :], X[:, TPC * c + j, :], j)
                        last.then_inc(x2n_ready, 1)
                    elif kind == "x_turn":
                        dve.wait_ge(x2n_turned, c + 1)
                        nc.vector.tensor_copy(X2T[:, c * CH:(c + 1) * CH], PS[:, MISC, :]).then_inc(x2t_ready, 1)
                if not last_group:
                    assert count[0] == LINKS_G

            with dve.Fori(0, G - 1) as g:
                group(g, BODY, False)
            group(G - 1, LAST, True)

            start = base[0] + count[0]
            LINKS_M = 3
            with dve.Fori(0, NC) as c:
                base[0], count[0] = start + LINKS_M * c, 0
                for m in range(FT):
                    dve.wait_ge(silu_done, FT * c + m + 1)
                    nc.vector.scalar_tensor_tensor(out=hA[:, m, :], in0=PS[:, 2 * (m % 2) + 1, :],
                                                   scalar=scales[:, 1, m:m + 1], in1=silu[:, m % 2, :],
                                                   op0=ALU.mult, op1=ALU.mult).then_inc(up_used, 1)
                dve.wait_ge(y_ready, c + 1)
                nc.vector.tensor_tensor(yb[:, :, :], PS[:, 4:8, 0:C],
                                        s3[:, :].unsqueeze(1).broadcast_to([P, TPC, C]),
                                        ALU.mult).then_inc(y_used, 1)
                dve.wait_ge(y_used, c + 1 + BASE)
                norm_stats(lambda j: yb[:, j, :], 3 * NC + c + 1)
                for j in range(TPC):
                    last = normed(yn[:, j, :], yb[:, j, :], j)
                link(last)
                dve.wait_ge(o_stored, 16 * c + BASE)
                nc.vector.tensor_tensor(ob[:, :, :], X[:, bass.ds(TPC * c, TPC), :], yn[:, :, :],
                                        ALU.add).then_inc(o_ready, 1)


def rope_tables():
    inv_freq = (1.0 / np.float32(ROPE_BASE) ** (np.arange(0, D, 2, dtype=np.float32) / D)).astype(np.float32)
    freqs = (np.arange(T, dtype=np.float32)[:, None] * inv_freq[None, :]).astype(np.float64)
    scale = 1.0 / np.sqrt(D)
    tables = np.stack([np.stack([f(freqs) * scale, f(freqs)], 1) for f in (np.cos, np.sin)], 1)
    tables = tables.reshape(T // P, P, 4 * D // 2).transpose(1, 0, 2)
    return np.ascontiguousarray(tables.reshape(P, -1), dtype=np.float32)


def kernel(L0_attn_x, L0_attn_Wq, L0_attn_bq, L0_attn_Wk, L0_attn_bk, L0_attn_Wv, L0_attn_bv, L0_attn_Wo,
           L0_attn_bo, L0_ffn_w1_w, L0_ffn_w1_s, L0_ffn_w2_w, L0_ffn_w2_s, L0_ffn_h1_w, L0_ffn_h1_s,
           L0_ffn_h2_w, L0_ffn_h2_s, L0_ffn_w3_w, L0_ffn_w3_s):
    import ml_dtypes
    import concourse.bacc as bacc
    from concourse.bass_utils import run_bass_kernel_spmd

    def lay(a):
        return np.ascontiguousarray(a)

    def columns(s):
        return np.asarray(s).reshape(FT, P).T

    tri = np.where(np.arange(P)[None, :] > np.arange(P)[:, None], np.float32(LOWEST), np.float32(0))
    arrays = {
        "x": lay(np.asarray(L0_attn_x).reshape(T, C)),
        "wqkv": lay(np.concatenate([np.asarray(w).T for w in (L0_attn_Wq, L0_attn_Wk, L0_attn_Wv)], 1)),
        "bqkv": lay(np.concatenate([np.asarray(b) for b in (L0_attn_bq, L0_attn_bk, L0_attn_bv)])[None, :]),
        "wo": lay(np.asarray(L0_attn_Wo).T),
        "bo": lay(np.asarray(L0_attn_bo)[None, :]),
        "w12": lay(np.concatenate([np.asarray(L0_ffn_w1_w).T, np.asarray(L0_ffn_w2_w).T], 1)),
        "h1": lay(np.asarray(L0_ffn_h1_w).T),
        "h2": lay(np.asarray(L0_ffn_h2_w).T),
        "w3": lay(np.asarray(L0_ffn_w3_w).T),
        "scales": lay(np.concatenate([columns(s) for s in (L0_ffn_w1_s, L0_ffn_w2_s, L0_ffn_h1_s,
                                                           L0_ffn_h2_s)], 1)),
        "s3": lay(np.asarray(L0_ffn_w3_s)[None, :]),
        "ident": np.eye(P, dtype=np.float32),
        "mask": lay(np.concatenate([np.zeros((P, CH - P), np.float32), tri], 1)),
        "rope": rope_tables(),
        "ones": np.ones((PARTS, COLS), ml_dtypes.bfloat16),
    }
    nc = bacc.Bacc("TRN2", target_bir_lowering=False, num_devices=1)
    args = [nc.dram_tensor(f"in_{n}", a.shape, mybir.dt.from_np(a.dtype), kind="ExternalInput").ap()
            for n, a in arrays.items()]
    out = nc.dram_tensor("out_y", (T, C), mybir.dt.float32, kind="ExternalOutput").ap()
    attention_mlp_kernel(nc, *args, out)
    r = run_bass_kernel_spmd(nc, [{f"in_{n}": a for n, a in arrays.items()}], core_ids=[0])
    return r.results[0]["out_y"].reshape(1, T, C)
```

```python
import numpy as np

import concourse.bass as bass
from concourse import mybir
from contextlib import ExitStack

T = 2048
C = 128
H = 16
D = C // H
P = 128
HG = 4
G = H // HG
CH = 512
NC = T // CH
TPC = CH // P
F = 512
FT = F // P
PARTS = 3
KR = PARTS * PARTS * D
VW = D + 1
EPS = 1e-5
LOWEST = -3.0e38
ROPE_BASE = 10000.0
COLS = NC * HG * CH
STEPS = sum(TPC * (c + 1) for c in range(NC))
FIRST_STEP = [sum(TPC * (b + 1) for b in range(c)) for c in range(NC)]
FIRST_PIECE = [sum(HG * TPC * (b + 1) for b in range(c)) for c in range(NC)]
PIECES = sum(HG * TPC * (c + 1) for c in range(NC))
RING = 4
NEG_AT = 2
RINGED = PIECES + NC
MAXBANKS = 3
BASE = 1

CUT_CHUNK = 2
LAG = 3
PACE = 24


def steps_of(dg, chunks):
    return [(dg, c, kt, max(0, kt - TPC * c) * P) for c in chunks for kt in range(TPC * (c + 1))]


def piece_at(c, kc, h, qt):
    n = (kc * HG + h) * TPC + qt
    return FIRST_PIECE[c] + c + n + (1 if n >= NEG_AT else 0)


def neg_at(c):
    return FIRST_PIECE[c + 1] + c + 1 + NEG_AT


def neg_passage(grp, c):
    if c < NC - 1:
        return neg_at(c), neg_at(c) % MAXBANKS
    return RINGED + (0 if isinstance(grp, int) and grp == G - 1 else NEG_AT), NEG_AT % MAXBANKS


def passed_before(grp, at):
    if isinstance(grp, int) and grp == 0 and at <= NEG_AT:
        return at
    return RINGED * grp + at - 1


CUT_AT = piece_at(NC - 1, 1, 0, 0)


def passages(dg, first, last):
    every = {piece_at(c, kc, h, qt): (dg, c, h, qt, kc) for c in range(NC) for kc in range(c + 1)
             for h in range(HG) for qt in range(TPC)}
    every.update({neg_at(c): (dg, c) for c in range(NC - 1)})
    every[NEG_AT] = (dg - 1, NC - 1)
    return [every[n] for n in range(first, min(last, RINGED))]


def order(carried, steps, ring, mlp_input=False):
    steps, in_loop = carried + steps, steps[-1][0] == 1
    pv_steps = steps if mlp_input else steps[:-LAG]
    hop = 0.19
    lists = {"pe": [], "act": [], "dve": [], "pool": [], "sp": []}
    t = {"pe": 0.0, "act": 0.0, "dve": 0.0}
    small, dve_due, sp_due = [], [], []
    exp_end, pv_end, used = {n: 0.0 for n in range(2 * len(carried))}, {}, []
    loaded, negated = {}, {}
    st, pv, at = HG * len(carried), 0, 0
    free = {"o": None if carried else 0.0, "vg": 0.0, "rows": 0.0}
    finished = [(0.0, c) for c in range(CUT_CHUNK - 1)] if mlp_input else []

    def on(engine, item, ready, cost):
        start = max(t[engine], ready)
        t[engine] = start + cost
        lists[engine].append(item)
        return t[engine]

    def dve_task(item, ready):
        kind, dg, c = item
        cost = {"o_norm": 0.5, "vg": 0.4, "a_copy": 0.6, "y_stats": 2.2, "x_stats": 3.2, "x_norm": 1.1,
                "x_copy": 0.6}[kind]
        end = on("dve", item, ready, cost)
        if kind == "vg":
            free["vg"] = end + hop
        elif kind == "o_norm":
            free["o"] = end + hop
            if c < NC - 1:
                finished.append((end + hop, c))
        elif kind == "a_copy":
            small.append((end + hop, ("a_proj", dg, c)))
        elif kind in ("y_stats", "x_stats"):
            lists["pool"].append(("rsqrt", dg, c, 0 if kind == "y_stats" else 1))
            dve_due.append((end + 1.3, ("x_stats" if kind == "y_stats" else "x_norm", dg, c)))
        elif kind == "x_norm":
            small.append((end + hop, ("x_turn", dg, c)))
        elif kind == "x_copy":
            free["rows"] = end + hop

    def dve_catch_up(now):
        while dve_due and min(dve_due)[0] <= max(now, t["dve"]):
            due = min(dve_due)
            dve_due.remove(due)
            dve_task(due[1], due[0])

    if in_loop:
        for c in range(CUT_CHUNK):
            sp_due.append((0.0, ("q", 1, c)))
            loaded["q", 1, c] = 3.0 * (c + 1)
        for c in range(NC):
            if piece_at(NC - 1, c, HG - 1, TPC - 1) < CUT_AT:
                sp_due.append((0.0, ("km", 1, c)))
                loaded["km", 1, c] = 9.0
    while True:
        dve_catch_up(t["pe"])
        if mlp_input and finished and free["rows"] is not None and at == len(ring):
            ready, c = finished.pop(0)
            small.append((max(ready, free["rows"], used[-1] + hop), ("a_turn", 0, c)))
            free["rows"] = None
        found = []
        if small:
            ready, item = min(small)
            found.append((ready, 0, "small", item))
        if at < len(ring):
            ready = used[at - MAXBANKS] + hop if at >= MAXBANKS else 0.0
            if len(ring[at]) == 2:
                found.append((max(ready, negated.get(ring[at], 0.0)), 1, "neg_turn", ring[at]))
            else:
                dg, c, h, qt, kc = ring[at]
                ready = max(ready, loaded.get(("q", dg, c), 0.0), loaded.get(("km", dg, kc), 0.0))
                ahead = at - (st - HG * len(carried))
                waiting = sum(u > t["pe"] for u in used[-MAXBANKS:])
                rank = 1 if (waiting < 1 and ahead < PACE) or ahead < PACE - 2 else 4
                found.append((ready, rank, "piece", ring[at]))
        if st < HG * len(steps):
            i, h = divmod(st, HG)
            if i < pv + RING:
                s = steps[i]
                ready = exp_end[st // 2 - 2] + hop if st >= HG else 0.0
                if s[2] == 0:
                    ready = max(ready, loaded.get(("neg", s[0], s[1]), 0.0), loaded.get(("ke", s[0], s[1]), 0.0))
                    if ("neg", s[0], s[1]) not in loaded and any(p[:2] == s[:2] for p in ring):
                        ready = None
                if ready is not None:
                    found.append((ready, 2 if t["act"] < t["pe"] + 2.0 else 3.5, "st", (s, h)))
        if pv < len(pv_steps) and 2 * pv + 1 in exp_end:
            s = pv_steps[pv]
            ready = exp_end[2 * pv + 1] + hop + (1.3 if s[2] >= TPC * s[1] else 0.0)
            if s[2] == 0:
                first = s[1] == 0
                if free["o"] is None or (first and free["vg"] is None):
                    ready = None
                else:
                    ready = max(ready, free["o"], free["vg"] if first else 0.0)
            if ready is not None:
                found.append((ready, 3, "pv", s))
        if not found:
            if not dve_due:
                break
            due = min(dve_due)
            dve_due.remove(due)
            dve_task(due[1], due[0])
            continue
        start, _, kind, item = min(found, key=lambda f: (max(f[0], t["pe"]), f[1]))
        if dve_due and min(dve_due)[0] < start and start > t["pe"]:
            t["pe"] = max(t["pe"], min(dve_due)[0])
            dve_catch_up(t["pe"])
            continue
        if kind == "small":
            small.remove(min(small))
            end = on("pe", item, start, 0.45)
            follow = {"o_turn": "o_norm", "a_turn": "a_copy", "a_proj": "y_stats", "x_turn": "x_copy"}[item[0]]
            dve_due.append((end + hop, (follow,) + item[1:]))
        elif kind == "neg_turn":
            at += 1
            end = on("pe", ("neg_turn",) + item, start, 0.06)
            used.append(on("dve", ("neg_copy",) + item, end + hop, 0.13))
            loaded[("neg",) + item] = used[-1] + 2.5
            sp_due.append((used[-1], ("neg",) + item))
        elif kind == "piece":
            dg, c, h, qt, kc = item
            at += 1
            width = CH if kc < c else (qt + 1) * P
            end = on("pe", ("piece",) + item, start, 0.003 + 0.213 * width / CH)
            used.append(on("dve", ("piece",) + item, end + hop, 0.07 + 0.00104 * width))
            if (h, qt) == (HG - 1, TPC - 1):
                if kc == c:
                    negated[dg, c] = on("dve", ("neg_split", dg, c), 0.0, 0.8) + hop
                if in_loop and dg == 0 and c == NC - 1:
                    sp_due.append((end, ("km", 1, kc)))
                    loaded["km", 1, kc] = end + 3.0
        elif kind == "st":
            s, h = item
            n = st // 2
            cols = CH - s[3]
            end = on("pe", ("st",) + s + (h,), start, 0.003 + 0.213 * cols / CH)
            st += 1
            if h % 2 == 1:
                slot_free = pv_end[n // 2 - RING] + hop if n // 2 >= RING else 0.0
                exp_end[n] = on("act", ("exp",) + s + (h // 2,), max(end + hop, slot_free), 0.05 + 0.00167 * cols)
            if h == HG - 1:
                dg, c, kt, _ = s
                if kt >= TPC * c:
                    lists["pool"].append(("mask",) + s)
                if kt == TPC * (c + 1) - 1 and c >= CUT_CHUNK:
                    sp_due.append((end, ("q", dg + 1, c)))
                    loaded["q", dg + 1, c] = end + 3.0
                if c == NC - 1 and kt % TPC == TPC - 1:
                    sp_due.append((end, ("ke", dg + 1, kt // TPC)))
                    loaded["ke", dg + 1, kt // TPC] = end + 3.0
        else:
            dg, c, kt, off = item
            pv_end[pv] = on("pe", ("pv",) + item, start, 0.06 + 0.00167 * (CH - off))
            if kt == 0:
                free["o"] = None
            if kt == TPC * (c + 1) - 1:
                done = on("act", ("o_copy", dg, c), pv_end[pv] + hop, 0.5)
                small.append((done + hop, ("o_turn", dg, c)))
                if c == NC - 1 and not mlp_input:
                    free["vg"] = None
                    dve_due.append((pv_end[pv] + hop, ("vg", dg + 1, 0)))
            pv += 1
    lists["sp"] = [item for _, item in sorted(sp_due)]
    return lists


FIRST_HALF = steps_of(0, range(CUT_CHUNK))
START = order([], FIRST_HALF, [e for e in passages(0, 0, CUT_AT) if e[0] == 0])
for tile in range(TPC):
    START["pe"].insert(MAXBANKS + 3 * tile, ("parts_turn", 0, tile))
START["dve"].insert(START["dve"].index(("neg_split", 0, 0)) + 1, ("o_clear", 0, 0))
LOOP = order(FIRST_HALF[-LAG:], steps_of(0, range(CUT_CHUNK, NC)) + steps_of(1, range(CUT_CHUNK)),
             passages(0, CUT_AT, RINGED) + passages(1, 0, CUT_AT))
END = order(FIRST_HALF[-LAG:], steps_of(0, range(CUT_CHUNK, NC)), passages(0, CUT_AT, RINGED)
            + [(0, NC - 1)], True)


def attention_mlp_kernel(nc, x_in, wqkv_in, bqkv_in, wo_in, bo_in, w12_in, h1_in, h2_in, w3_in,
                         scales_in, s3_in, ident_in, mask_in, rope_in, ones_in, out_dram):
    f32, bf16 = mybir.dt.float32, mybir.dt.bfloat16
    ALU, ACT, AX = mybir.AluOpType, mybir.ActivationFunctionType, mybir.AxisListType

    parts_dram = nc.dram_tensor("parts_dram", [2, NC, PARTS, D, H * CH], bf16, kind="Internal").ap()

    ctx = ExitStack()
    with ctx:
        def sb(name, shape, dt=f32):
            return ctx.enter_context(nc.sbuf_tensor(name, shape, dt))

        def sem(name):
            return ctx.enter_context(nc.semaphore(name))

        QA = sb("QA", [P, COLS], bf16)
        KM = sb("KM", [P, COLS], bf16)
        KE = sb("KE", [P, COLS], bf16)
        PR = sb("PR", [P, RING, HG, CH])
        VA = sb("VA", [P, G, T // P, HG, VW])
        VG = sb("VG", [P, T // P, HG, VW])
        X = sb("X", [P, T // P, C])
        AT = sb("AT", [P, T // P, C])
        OT = sb("OT", [P, CH])
        work = sb("work", [P, 5632])
        XN = sb("XN", [P, TPC, C])
        XT = sb("XT", [P, CH])
        pieces3 = sb("pieces3", [P, TPC, PARTS, 2 * C], bf16)
        piecesT = sb("piecesT", [P, 2 * PARTS, CH], bf16)
        wqkv = sb("wqkv", [P, 3 * C])
        bqkv = sb("bqkv", [P, 3 * C])
        wo = sb("wo", [P, C])
        bo = sb("bo", [P, C])
        s3 = sb("s3", [P, C])
        scales = sb("scales", [P, 4, FT])
        ident = sb("ident", [P, P])
        identb = sb("identb", [P, P], bf16)
        mask = sb("mask", [P, CH])
        rope = sb("rope", [P, T // P, 2, 2, D // 2])
        junk = sb("junk", [P, 4, CH], bf16)
        mpart = sb("mpart", [P, HG * TPC, NC])
        mx = sb("mx", [P, HG * TPC])
        mres = sb("mres", [P, HG * TPC])
        mneg = sb("mneg", [P, P], bf16)
        mT = sb("mT", [P, NC, P], bf16)
        rec = sb("rec", [P, TPC * HG])
        stats = sb("stats", [P, TPC, 6])
        mv = sb("mv", [P, TPC, 2])
        var = sb("var", [P, TPC])
        rstd = sb("rstd", [P, TPC])
        nhalf = sb("nhalf", [P, TPC])
        yb = sb("yb", [P, TPC, C])
        yn = sb("yn", [P, TPC, C])
        ob = sb("ob", [P, TPC, C])
        silu = sb("silu", [P, 2, CH])
        aT = sb("aT", [P, CH])
        X2T = sb("X2T", [P, T])

        def tile2(at):
            return work[:, at:at + TPC * 2 * C].rearrange("p (j n) -> p j n", j=TPC)

        qk, ra, rb, qr, qres = (tile2(n * TPC * 2 * C) for n in range(5))
        at = 5 * TPC * 2 * C
        xstats = work[:, at:at + 6 * T // P].rearrange("p (t n) -> p t n", n=6)
        xmv = work[:, at + 6 * T // P:at + 8 * T // P].rearrange("p (t n) -> p t n", n=2)
        xvar = work[:, at + 8 * T // P:at + 9 * T // P]
        xrstd = work[:, at + 9 * T // P:at + 10 * T // P]
        xhalf = work[:, at + 10 * T // P:at + 11 * T // P]
        w12 = work[:, 0:2 * F].rearrange("p (a n) -> p a n", a=2)
        h1 = work[:, 2 * F:2 * F + FT * F].rearrange("p (k n) -> p k n", k=FT)
        h2 = work[:, 2 * F + FT * F:2 * F + 2 * FT * F].rearrange("p (k n) -> p k n", k=FT)
        w3 = work[:, 2 * F + 2 * FT * F:].rearrange("p (k n) -> p k n", k=FT)
        hA, hB, hC = PR[:, 0], PR[:, 1], PR[:, 2]

        PS = ctx.enter_context(nc.psum_tensor("PS", [P, 8, CH], f32))
        MAXB, OB, MISC = 4, 7, 6


        def parts_bank(c, j):
            first = 0 if isinstance(c, int) and c == NC - 1 else MISC
            return PS[:, first if j % 2 == 0 else OB, :].bitcast(bf16)[:, 0:2 * PARTS * P]

        x_loaded, w_loaded, c_loaded = sem("x_loaded"), sem("w_loaded"), sem("c_loaded")
        idb_ready = sem("idb_ready")
        q_padded, k_padded = sem("q_padded"), sem("k_padded")
        xvar_ready, xrstd_ready = sem("xvar_ready"), sem("xrstd_ready")
        var_ready, rstd_ready, xn_ready = sem("var_ready"), sem("rstd_ready"), sem("xn_ready")
        xn_turned, xt_ready, qkv_ready = sem("xn_turned"), sem("xt_ready"), sem("qkv_ready")
        qk_ready, ra_ready, qr_ready = sem("qk_ready"), sem("ra_ready"), sem("qr_ready")
        rb_ready = sem("rb_ready")
        hi_ready, res_ready, mid_ready = sem("hi_ready"), sem("res_ready"), sem("mid_ready")
        lo_ready, pt_turned, pt_copied = sem("lo_ready"), sem("pt_turned"), sem("pt_copied")
        pt_stored = sem("pt_stored")
        nh_ready = sem("nh_ready")
        q_loaded = [sem(f"q_loaded{c}") for c in range(NC)]
        km_loaded = [sem(f"km_loaded{c}") for c in range(NC)]
        ke_loaded = [sem(f"ke_loaded{c}") for c in range(NC)]
        negs_loaded = [sem(f"negs_loaded{c}") for c in range(NC)]
        ones_loaded = sem("ones_loaded")
        ps_ready, ps_used = sem("piece_ready"), sem("piece_used")
        neg_ready = sem("neg_ready")
        o_clear = sem("o_clear")
        st_ready, exp_done, masked = sem("scores_ready"), sem("exp_done"), sem("masked")
        vg_ready, pv_done = sem("vg_ready"), sem("pv_done")
        o_copied, o_turned = sem("o_copied"), sem("o_turned")
        at_ready, a_turned, aT_ready = sem("at_ready"), sem("a_turned"), sem("aT_ready")
        proj_ready, proj_used = sem("proj_ready"), sem("proj_used")
        x2n_ready, x2n_turned = sem("x2n_ready"), sem("x2n_turned")
        x2t_ready = sem("x2t_ready")
        mlp_loaded = sem("mlp_loaded")
        up_ready, silu_done, up_used = sem("up_ready"), sem("silu_done"), sem("up_used")
        g1_in, g1_done, g2_in, g2_done = sem("g1_in"), sem("g1_done"), sem("g2_in"), sem("g2_done")
        y_ready, y_used, o_ready, o_stored = sem("y_ready"), sem("y_used"), sem("o_ready"), sem("o_stored")
        vstep = sem("vstep")

        alone = sem("alone")
        from_base = [xn_turned, qk_ready, pt_copied, qkv_ready, pt_turned, pt_stored, lo_ready, y_used, g2_done, up_used, o_stored] + negs_loaded

        block = ctx.enter_context(nc.Block())

        @block.sync
        def _(sp):
            for s in from_base:
                sp.sem_inc(s, BASE)
            sp.dma_start(X[:, :, :], x_in.rearrange("(t p) f -> p t f", p=P)).then_inc(x_loaded, 16)
            sp.dma_start(ident[:, :], ident_in).then_inc(w_loaded, 16)
            sp.dma_start(wqkv[:, :], wqkv_in).then_inc(w_loaded, 16)
            sp.dma_start(bqkv[:, :], bqkv_in.broadcast_to([P, 3 * C])).then_inc(w_loaded, 16)
            sp.dma_start(rope[:, :, :, :, :].rearrange("p t a b f -> p (t a b f)"), rope_in).then_inc(w_loaded, 16)
            sp.dma_start(mask[:, :], mask_in).then_inc(c_loaded, 16)
            sp.dma_start(wo[:, :], wo_in).then_inc(c_loaded, 16)
            sp.dma_start(bo[:, :], bo_in.broadcast_to([P, C])).then_inc(c_loaded, 16)
            sp.dma_start(s3[:, :], s3_in.broadcast_to([P, C])).then_inc(c_loaded, 16)
            sp.dma_start(scales[:, :, :].rearrange("p a m -> p (a m)"), scales_in).then_inc(c_loaded, 16)
            sp.wait_ge(q_padded, 1)
            sp.wait_ge(k_padded, 2)
            sp.dma_start(KE[KR:KR + PARTS, :], ones_in).then_inc(ones_loaded, 16)

            def load_q(g, c):
                for a in range(PARTS):
                    q = parts_dram[0, c, a, :, bass.ds(g * HG * CH, HG * CH)]
                    sp.dma_start(QA[a * PARTS * D:(a + 1) * PARTS * D, c * HG * CH:(c + 1) * HG * CH],
                                 q.unsqueeze(0).broadcast_to([PARTS, D, HG * CH])).then_inc(q_loaded[c], 16)

            def load_k(dst, loaded, g, c):
                for a in range(PARTS):
                    k = parts_dram[1, c, :, :, bass.ds(g * HG * CH, HG * CH)]
                    sp.dma_start(dst[a * PARTS * D:(a + 1) * PARTS * D, c * HG * CH:(c + 1) * HG * CH],
                                 k).then_inc(loaded[c], 16)

            def load_negs(g, c):
                sp.wait_ge(ps_used, passed_before(g, neg_passage(g, c)[0]) + 1)
                sp.sem_inc(alone, 1)
                rows = QA[KR:KR + PARTS, c * HG * CH:(c + 1) * HG * CH]
                sp.dma_start(rows.rearrange("p (a s) -> p a s", s=P),
                             mT[0:PARTS * HG * TPC, c, :]).then_inc(negs_loaded[c], 16)

            for c in range(NC):
                sp.wait_ge(pt_copied, TPC * (c + 1) + BASE)
                for i in range(2 * PARTS):
                    sp.dma_start(parts_dram[i // PARTS, c, i % PARTS].rearrange("d (h s) -> h d s", h=H),
                                 piecesT[:, i, :]).then_inc(pt_stored, 16)
                if c == NC - 1:
                    load_negs(0, 0)
                sp.wait_ge(pt_stored, 96 * (c + 1) + BASE)
                load_q(0, c)
                load_k(KM, km_loaded, 0, c)
                load_k(KE, ke_loaded, 0, c)
            def stretch(g, items):
                for kind, dg, c in items:
                    if kind == "neg":
                        load_negs(g + dg, c)
                    elif kind == "q":
                        sp.wait_ge(st_ready, 2 * (STEPS * (g + dg - 1) + FIRST_STEP[c] + TPC * (c + 1)))
                        sp.sem_inc(alone, 1)
                        load_q(g + dg, c)
                    elif kind == "ke":
                        sp.wait_ge(st_ready, 2 * (STEPS * (g + dg - 1) + FIRST_STEP[NC - 1] + TPC * (c + 1)))
                        sp.sem_inc(alone, 1)
                        load_k(KE, ke_loaded, g + dg, c)
                    elif kind == "km":
                        last = passed_before(g + dg - 1, piece_at(NC - 1, c, HG - 1, TPC - 1))
                        sp.wait_ge(ps_ready, last + 1)
                        sp.sem_inc(alone, 1)
                        load_k(KM, km_loaded, g + dg, c)

            stretch(0, [item for item in START["sp"] if item != ("neg", 0, 0)])
            with sp.Fori(0, G - 1) as g:
                stretch(g, LOOP["sp"])
            stretch(G - 1, [item for item in END["sp"] if item[0] == "neg"])
            sp.dma_start(w12[:, :, :].rearrange("p a n -> p (a n)"), w12_in).then_inc(mlp_loaded, 16)
            sp.dma_start(h1, h1_in.rearrange("(k p) n -> p k n", p=P)).then_inc(mlp_loaded, 16)
            sp.dma_start(h2, h2_in.rearrange("(k p) n -> p k n", p=P)).then_inc(mlp_loaded, 16)
            sp.dma_start(w3, w3_in.rearrange("(k p) n -> p k n", p=P)).then_inc(mlp_loaded, 16)
            with sp.Fori(0, NC) as c:
                sp.wait_ge(o_ready, c + 1)
                sp.dma_start(out_dram[bass.ds(c * CH, CH), :].rearrange("(j p) f -> p j f", p=P),
                             ob[:, :, :]).then_inc(o_stored, 16)
            sp.wait_ge(o_stored, 16 * NC + BASE)

        @block.tensor
        def _(pe):
            pe.wait_ge(w_loaded, 64)
            pe.wait_ge(idb_ready, 1)

            def x_turn(c):
                pe.wait_ge(xn_ready, c + 1)
                for j in range(TPC):
                    last = nc.tensor.transpose(PS[:, MAXB, j * P:(j + 1) * P], XN[:, j, :], ident[:, :])
                last.then_inc(xn_turned, 1)

            def qkv(c):
                pe.wait_ge(xt_ready, c + 1)
                for j in range(TPC):
                    if not isinstance(c, int):
                        pe.wait_ge(qk_ready, TPC * (c - 1) + j + 1 + BASE)
                    nc.tensor.matmul(PS[:, j, 0:3 * C], XT[:, j * P:(j + 1) * P], wqkv[:, :],
                                     start=True, stop=True).then_inc(qkv_ready, 1)

            def parts_turn(c, j):
                pe.wait_ge(lo_ready, TPC * c + j + 1 + BASE)
                if j >= 2:
                    pe.wait_ge(pt_copied, TPC * c + j - 1 + BASE)
                else:
                    pe.wait_ge(pt_copied, TPC * c + BASE)
                for i in range(2 * PARTS):
                    a = i // PARTS
                    last = nc.tensor.transpose(parts_bank(c, j)[:, i * P:(i + 1) * P],
                                               pieces3[:, j, i % PARTS, a * C:(a + 1) * C], identb[:, :])
                last.then_inc(pt_turned, 1)

            x_turn(0)
            qkv(0)
            with pe.Fori(0, NC - 1) as c:
                x_turn(c + 1)
                qkv(c + 1)
                for j in range(TPC):
                    parts_turn(c, j)

            def ring_free(grp, at):
                if at >= MAXBANKS:
                    pe.wait_ge(ps_used, passed_before(grp, at - MAXBANKS) + 1)
                elif not (isinstance(grp, int) and grp == 0):
                    pe.wait_ge(ps_used, passed_before(grp, 0))

            def stretch(g, items):
                for item in items:
                    kind, c = item[0], item[2]
                    grp = g + item[1]
                    if kind == "parts_turn":
                        parts_turn(NC - 1, c)
                    elif kind == "piece":
                        _, _, _, h, qt, kc = item
                        at = piece_at(c, kc, h, qt)
                        if (h, qt, kc) == (0, 0, 0):
                            pe.wait_ge(q_loaded[c], 48 * (grp + 1))
                        if (h, qt, kc) == (0, 0, c):
                            pe.wait_ge(km_loaded[c], 48 * (grp + 1))
                        ring_free(grp, at)
                        width = CH if kc < c else (qt + 1) * P
                        q0, k0 = (c * HG + h) * CH + qt * P, (kc * HG + h) * CH
                        nc.tensor.matmul(PS[:, MAXB + at % MAXBANKS, 0:width], QA[:, q0:q0 + P],
                                         KM[:, k0:k0 + width], start=True, stop=True).then_inc(ps_ready, 1)
                    elif kind == "neg_turn":
                        pe.wait_ge(neg_ready, NC * grp + c + 1)
                        at, bank = neg_passage(grp, c)
                        ring_free(grp, at)
                        pe.sem_inc(alone, 1)
                        nc.tensor.transpose(PS[:, MAXB + bank, :].bitcast(bf16)[:, 0:P],
                                            mneg[:, :], identb[:, :]).then_inc(ps_ready, 1)
                    elif kind == "st":
                        _, _, _, kt, off, h = item
                        if kt == 0 and h == 0:
                            pe.wait_ge(negs_loaded[c], 16 * (grp + 1) + BASE)
                            pe.wait_ge(ke_loaded[c], 48 * (grp + 1))
                            if c == 0:
                                pe.wait_ge(ones_loaded, 16)
                        n = 2 * (FIRST_STEP[c] + kt) + h // 2
                        if h % 2 == 0 and not (isinstance(grp, int) and grp == 0 and n < 2):
                            pe.wait_ge(exp_done, 2 * STEPS * grp + n - 1)
                        k0 = (kt // TPC * HG + h) * CH + kt % TPC * P
                        q0 = (c * HG + h) * CH + off
                        last = nc.tensor.matmul(PS[:, h, off:CH], KE[:, k0:k0 + P],
                                                QA[:, q0:q0 + CH - off], start=True, stop=True)
                        if h % 2 == 1:
                            last.then_inc(st_ready, 1)
                    elif kind == "pv":
                        _, _, _, kt, off = item
                        step = FIRST_STEP[c] + kt
                        if kt >= TPC * c:
                            pe.wait_ge(masked, NC * TPC * grp + TPC * c + kt - TPC * c + 1)
                        else:
                            pe.wait_ge(exp_done, 2 * (STEPS * grp + step + 1))
                        if kt == 0 and c == 0:
                            pe.wait_ge(vg_ready, grp + 1)
                            pe.wait_ge(o_clear, 1)
                        if kt == 0 and not (isinstance(grp, int) and grp == 0 and c == 0):
                            pe.wait_ge(at_ready, NC * grp + c)
                        for h in range(HG):
                            last = nc.tensor.matmul(PS[32 * h:32 * h + VW, OB, off:CH], VG[:, kt, h, :],
                                                    PR[:, step % RING, h, off:CH], start=(kt == 0),
                                                    stop=(kt == TPC * (c + 1) - 1))
                        last.then_inc(pv_done, 1)
                    elif kind == "o_turn":
                        pe.wait_ge(o_copied, NC * grp + c + 1)
                        for j in range(TPC):
                            last = nc.tensor.transpose(PS[:, OB, j * P:(j + 1) * P],
                                                       OT[:, j * P:(j + 1) * P], ident[:, :])
                        last.then_inc(o_turned, 1)
                    elif kind == "a_turn":
                        if c == 0:
                            pe.wait_ge(ps_used, passed_before(G - 1, RINGED) + 1)
                        else:
                            pe.wait_ge(x2t_ready, c)
                        a_turn(c)
                    elif kind == "a_proj":
                        a_proj(c)
                    elif kind == "x_turn":
                        x2_turn(c, MISC)

            def a_turn(c):
                pe.wait_ge(at_ready, NC * (G - 1) + c + 1)
                for j in range(TPC):
                    last = nc.tensor.transpose(PS[:, MISC, j * P:(j + 1) * P], AT[:, TPC * c + j, :], ident[:, :])
                last.then_inc(a_turned, 1)

            def a_proj(c):
                pe.wait_ge(aT_ready, c + 1)
                pe.wait_ge(c_loaded, 80)
                for j in range(TPC):
                    last = nc.tensor.matmul(PS[:, MISC, j * P:(j + 1) * P], aT[:, j * P:(j + 1) * P],
                                            wo[:, :], start=True, stop=True)
                last.then_inc(proj_ready, 1)

            def x2_turn(c, bank):
                pe.wait_ge(x2n_ready, c + 1)
                for j in range(TPC):
                    last = nc.tensor.transpose(PS[:, bank, j * P:(j + 1) * P], yn[:, j, :], ident[:, :])
                last.then_inc(x2n_turned, 1)

            stretch(0, START["pe"])
            with pe.Fori(0, G - 1) as g:
                stretch(g, LOOP["pe"])
            stretch(G - 1, END["pe"])

            def up(c, m):
                if m >= 2:
                    pe.wait_ge(up_used, FT * c + m - 1 + BASE)
                else:
                    pe.wait_ge(g2_done, FT * c + BASE)
                for a in range(2):
                    last = nc.tensor.matmul(PS[:, 2 * (m % 2) + a, :], w12[:, a, m * P:(m + 1) * P],
                                            X2T[:, bass.ds(c * CH, CH)], start=True, stop=True)
                last.then_inc(up_ready, 1)

            def hidden1(c, k):
                pe.wait_ge(up_used, FT * c + k + 1 + BASE)
                for m in range(FT):
                    last = nc.tensor.matmul(PS[:, 4 + m, :], h1[:, k, m * P:(m + 1) * P], hA[:, k, :],
                                            start=(k == 0), stop=(k == FT - 1))
                    if k == FT - 1:
                        last.then_inc(g1_in, 1)

            def hidden2_down(c):
                for k in range(FT):
                    pe.wait_ge(g1_done, FT * c + k + 1)
                    for m in range(FT):
                        last = nc.tensor.matmul(PS[:, m, :], h2[:, k, m * P:(m + 1) * P], hB[:, k, :],
                                                start=(k == 0), stop=(k == FT - 1))
                        if k == FT - 1:
                            last.then_inc(g2_in, 1)
                for k in range(FT):
                    pe.wait_ge(g2_done, FT * c + k + 1 + BASE)
                    for j in range(TPC):
                        last = nc.tensor.matmul(PS[:, 4 + j, 0:C], hC[:, k, j * P:(j + 1) * P], w3[:, k, :],
                                                start=(k == 0), stop=(k == FT - 1))
                last.then_inc(y_ready, 1)

            pe.wait_ge(x2t_ready, NC - 1)
            a_turn(NC - 1)
            pe.wait_ge(mlp_loaded, 64)
            up(0, 0)
            a_proj(NC - 1)
            for m in range(1, FT):
                up(0, m)
            pe.wait_ge(proj_used, NC)
            for k in range(FT):
                hidden1(0, k)
                if k == FT - 2:
                    pe.wait_ge(up_used, FT + BASE)
                    x2_turn(NC - 1, 0)
            pe.wait_ge(x2t_ready, NC)
            hidden2_down(0)
            with pe.Fori(0, NC - 1) as last_c:
                c = last_c + 1
                for m in range(FT):
                    up(c, m)
                pe.wait_ge(y_used, c + BASE)
                for k in range(FT):
                    hidden1(c, k)
                hidden2_down(c)

        @block.scalar
        def _(act):
            def x_copy(c):
                act.wait_ge(xn_turned, c + 1 + BASE)
                if not isinstance(c, int):
                    act.wait_ge(qkv_ready, TPC * c + BASE)
                nc.scalar.activation(XT[:, :], PS[:, MAXB, :], ACT.Copy).then_inc(xt_ready, 1)

            def parts(c):
                act.wait_ge(pt_turned, TPC * c + BASE)
                for j in range(TPC):
                    act.wait_ge(qr_ready, TPC * c + j + 1)
                    nc.scalar.activation(pieces3[:, j, 0, :], qr[:, j, :], ACT.Copy).then_inc(hi_ready, 1)
                for j in range(TPC):
                    act.wait_ge(res_ready, TPC * c + j + 1)
                    nc.scalar.activation(pieces3[:, j, 1, :], qres[:, j, :], ACT.Copy).then_inc(mid_ready, 1)
                act.wait_ge(pt_stored, 96 * c + BASE)
                for j in range(TPC):
                    act.wait_ge(pt_turned, TPC * c + j + 1 + BASE)
                    nc.scalar.activation(piecesT[:, :, j * P:(j + 1) * P],
                                         parts_bank(c, j).rearrange("p (i s) -> p i s", s=P), ACT.Copy).then_inc(pt_copied, 1)

            x_copy(0)
            with act.Fori(0, NC - 1) as c:
                x_copy(c + 1)
                parts(c)
            parts(NC - 1)

            def stretch(g, items):
                for item in items:
                    c, grp = item[2], g + item[1]
                    if item[0] == "exp":
                        _, _, _, kt, off, pr = item
                        step = FIRST_STEP[c] + kt
                        if pr == 0 and not (isinstance(grp, int) and grp == 0 and step < RING):
                            act.wait_ge(pv_done, STEPS * grp + step - RING + 1)
                        act.wait_ge(st_ready, 2 * (STEPS * grp + step) + pr + 1)
                        nc.scalar.activation(PR[:, step % RING, 2 * pr:2 * pr + 2, off:CH],
                                             PS[:, 2 * pr:2 * pr + 2, off:CH], ACT.Exp).then_inc(exp_done, 1)
                    else:
                        act.wait_ge(pv_done, STEPS * grp + FIRST_STEP[c] + TPC * (c + 1))
                        if not (isinstance(grp, int) and grp == 0 and c == 0):
                            act.wait_ge(o_turned, NC * grp + c)
                        nc.scalar.activation(OT[:, :], PS[:, OB, :], ACT.Copy).then_inc(o_copied, 1)

            stretch(0, START["act"])
            with act.Fori(0, G - 1) as g:
                stretch(g, LOOP["act"])
            stretch(G - 1, END["act"])

            with act.Fori(0, NC) as c:
                for m in range(FT):
                    act.wait_ge(up_ready, FT * c + m + 1)
                    if m >= 2:
                        act.wait_ge(up_used, FT * c + m - 1 + BASE)
                    else:
                        act.wait_ge(up_used, FT * c + BASE)
                    nc.scalar.activation(silu[:, m % 2, :], PS[:, 2 * (m % 2), :], ACT.Silu,
                                         scale=scales[:, 0, m:m + 1]).then_inc(silu_done, 1)
                for m in range(FT):
                    act.wait_ge(g1_in, FT * c + m + 1)
                    nc.scalar.activation(hB[:, m, :], PS[:, 4 + m, :], ACT.Gelu,
                                         scale=scales[:, 2, m:m + 1]).then_inc(g1_done, 1)
                for m in range(FT):
                    act.wait_ge(g2_in, FT * c + m + 1)
                    nc.scalar.activation(hC[:, m, :], PS[:, m, :], ACT.Gelu,
                                         scale=scales[:, 3, m:m + 1]).then_inc(g2_done, 1)

        @block.gpsimd
        def _(pool):
            nc.gpsimd.memset(nhalf[:, :], -0.5)
            nc.gpsimd.memset(xhalf, -0.5).then_inc(nh_ready, 1)
            pool.wait_ge(nh_ready, 1)
            for n, rows in enumerate((KM[P // 2:P, :], KE[P // 2:P, COLS // 2:COLS])):
                nc.gpsimd.memset(rows, 0.0).then_inc(k_padded, 1)
                pool.wait_ge(k_padded, n + 1)
            pool.wait_ge(w_loaded, 64)

            def rsqrt(n):
                pool.wait_ge(var_ready, n)
                nc.gpsimd.tensor_tensor(rstd[:, :], var[:, :], nhalf[:, :], ALU.pow).then_inc(rstd_ready, 1)

            def turned(c):
                for j in range(TPC):
                    pool.wait_ge(qk_ready, TPC * c + j + 1 + BASE)
                    cos = rope[:, bass.ds(TPC * c + j, 1), 0, :, :].rearrange("p t b f -> p (t b) f")
                    nc.gpsimd.tensor_tensor(
                        ra[:, j, :].rearrange("p (b h f) -> p b h f", b=2, f=D // 2),
                        qk[:, j, :].rearrange("p (b h f) -> p b h f", b=2, f=D // 2),
                        cos.unsqueeze(2).broadcast_to([P, 2, 2 * H, D // 2]), ALU.mult).then_inc(ra_ready, 1)

            def low_parts(c):
                for j in range(TPC):
                    pool.wait_ge(mid_ready, TPC * c + j + 1)
                    nc.gpsimd.tensor_tensor(pieces3[:, j, 2, :], qres[:, j, :], pieces3[:, j, 1, :],
                                            ALU.subtract).then_inc(lo_ready, 1)

            pool.wait_ge(xvar_ready, 1)
            nc.gpsimd.tensor_tensor(xrstd[:, 0:TPC], xvar[:, 0:TPC], xhalf[:, 0:TPC], ALU.pow).then_inc(xrstd_ready, 1)
            pool.wait_ge(xvar_ready, 2)
            nc.gpsimd.tensor_tensor(xrstd[:, TPC:T // P], xvar[:, TPC:T // P], xhalf[:, TPC:T // P],
                                    ALU.pow).then_inc(xrstd_ready, 1)
            with pool.Fori(0, NC) as c:
                turned(c)
                low_parts(c)

            def stretch(g, items):
                for item in items:
                    c, grp = item[2], g + item[1]
                    if item[0] == "rsqrt":
                        rsqrt(2 * c + item[3] + 1)
                    else:
                        _, _, _, kt, off = item
                        step = FIRST_STEP[c] + kt
                        pool.wait_ge(exp_done, 2 * (STEPS * grp + step + 1))
                        pool.sem_inc(alone, 1)
                        diag = PR[:, step % RING, :, off:off + P]
                        nc.gpsimd.affine_select(out=diag, in_=diag, compare_op=ALU.is_ge, fill=0.0, base=0,
                                                pattern=[[0, HG], [1, P]],
                                                channel_multiplier=-1).then_inc(masked, 1)

            stretch(0, START["pool"])
            with pool.Fori(0, G - 1) as g:
                stretch(g, LOOP["pool"])
            stretch(G - 1, END["pool"])
            rsqrt(2 * NC - 1)
            rsqrt(2 * NC)
            with pool.Fori(0, NC) as c:
                rsqrt(2 * NC + c + 1)

        @block.vector
        def _(dve):
            count, base = [0], [0]

            def link(ins):
                count[0] += 1
                ins.then_inc(vstep, 1)
                dve.wait_ge(vstep, base[0] + count[0])


            def norm_stats(src):
                for j in range(TPC):
                    last = nc.vector.bn_stats(stats[:, j, :], src(j))
                link(last)
                dve.sem_inc(alone, 1)
                for j in range(TPC):
                    last = nc.vector.bn_aggr(mv[:, j, :], stats[:, j, :])
                link(last)
                nc.vector.tensor_scalar(var[:, :], mv[:, :, 1], EPS, None, ALU.add).then_inc(var_ready, 1)

            def normed(dst, src, j):
                return nc.vector.tensor_scalar(dst, src, mv[:, j, 0:1], rstd[:, j:j + 1],
                                               ALU.subtract, ALU.mult)

            nc.vector.memset(QA[P // 2:P, :], 0.0)
            nc.vector.memset(KE[P // 2:P, 0:COLS // 2], 0.0).then_inc(q_padded, 1)
            nc.vector.memset(VA[:, :, :, :, D:VW].rearrange("p g t h v -> p (g t h) v"), 1.0)
            dve.wait_ge(w_loaded, 64)
            nc.vector.tensor_copy(identb[:, :], ident[:, :]).then_inc(idb_ready, 1)
            dve.wait_ge(x_loaded, 16)
            for n, tiles in enumerate((range(0, TPC), range(TPC, T // P))):
                for t in tiles:
                    last = nc.vector.bn_stats(xstats[:, t, :], X[:, t, :])
                link(last)
                for t in tiles:
                    last = nc.vector.bn_aggr(xmv[:, t, :], xstats[:, t, :])
                link(last)
                nc.vector.tensor_scalar(xvar[:, tiles[0]:tiles[-1] + 1], xmv[:, tiles[0]:tiles[-1] + 1, 1], EPS, None,
                                        ALU.add).then_inc(xvar_ready, 1)
            dve.wait_ge(xrstd_ready, 1)

            def x_normed(c):
                if not isinstance(c, int):
                    dve.wait_ge(xn_turned, c + BASE)
                for j in range(TPC):
                    t = bass.ds(TPC * c + j, 1)
                    last = nc.vector.tensor_scalar(XN[:, j, :], X[:, t, :].rearrange("p t f -> p (t f)"),
                                                   xmv[:, t, 0], xrstd[:, t], ALU.subtract, ALU.mult)
                last.then_inc(xn_ready, 1)

            def rotated(c):
                for step in range(TPC + 2):
                    j = step
                    if j < TPC:
                        dve.wait_ge(qkv_ready, TPC * c + j + 1 + BASE)
                        v = VA[:, :, bass.ds(TPC * c + j, 1), :, 0:D].rearrange("p g t h d -> p g (t h) d")
                        nc.vector.tensor_tensor(v, PS[:, j, 2 * C:3 * C].rearrange("p (g h d) -> p g h d", g=G, d=D),
                                                bqkv[:, 2 * C:3 * C].rearrange("p (g h d) -> p g h d", g=G, d=D),
                                                ALU.add)
                        nc.vector.tensor_tensor(qk[:, j, :], PS[:, j, 0:2 * C], bqkv[:, 0:2 * C],
                                                ALU.add).then_inc(qk_ready, 1)
                    j = step - 1
                    if 0 <= j < TPC:
                        dve.wait_ge(qk_ready, TPC * c + j + 1 + BASE)
                        halves = qk[:, j, :].rearrange("p (b h s f) -> p b h s f", b=2, s=2, f=D // 2)
                        turned = rb[:, j, :].rearrange("p (b h s f) -> p b h s f", b=2, s=2, f=D // 2)
                        sin = rope[:, bass.ds(TPC * c + j, 1), 1, :, :].rearrange("p t b f -> p (t b) f")
                        sin = sin.unsqueeze(2).broadcast_to([P, 2, H, D // 2])
                        nc.vector.tensor_tensor(turned[:, :, :, 0, :], halves[:, :, :, 1, :], sin, ALU.mult)
                        nc.vector.tensor_tensor(turned[:, :, :, 1, :], halves[:, :, :, 0, :], sin,
                                                ALU.mult).then_inc(rb_ready, 1)
                    j = step - 2
                    if 0 <= j < TPC:
                        dve.wait_ge(rb_ready, TPC * c + j + 1)
                        dve.wait_ge(ra_ready, TPC * c + j + 1)
                        a, b, r = (t[:, j, :].rearrange("p (n s f) -> p n s f", s=2, f=D // 2) for t in (ra, rb, qr))
                        nc.vector.tensor_tensor(r[:, :, 0, :], a[:, :, 0, :], b[:, :, 0, :], ALU.subtract)
                        nc.vector.tensor_tensor(r[:, :, 1, :], a[:, :, 1, :], b[:, :, 1, :],
                                                ALU.add).then_inc(qr_ready, 1)

            def residues(c):
                dve.wait_ge(lo_ready, TPC * c + BASE)
                for j in range(TPC):
                    dve.wait_ge(hi_ready, TPC * c + j + 1)
                    nc.vector.tensor_tensor(qres[:, j, :], qr[:, j, :], pieces3[:, j, 0, :],
                                            ALU.subtract).then_inc(res_ready, 1)

            x_normed(0)
            dve.wait_ge(xrstd_ready, 2)
            with dve.Fori(0, NC - 1) as c:
                x_normed(c + 1)
                rotated(c)
                residues(c)
            rotated(NC - 1)
            residues(NC - 1)

            nc.vector.memset(mneg[:, :], 0.0)
            dve.wait_ge(c_loaded, 80)

            def stretch(g, items, links):
                base[0], count[0] = links, 0
                for item in items:
                    kind, c = item[0], item[2]
                    grp = g + item[1]
                    if kind == "piece":
                        _, _, _, h, qt, kc = item
                        at = piece_at(c, kc, h, qt)
                        row = h * TPC + qt
                        dve.wait_ge(ps_ready, passed_before(grp, at) + 1)
                        if kc < c:
                            nc.vector.tensor_reduce(mpart[:, row, kc:kc + 1], PS[:, MAXB + at % MAXBANKS, :], AX.X,
                                                    ALU.max).then_inc(ps_used, 1)
                        else:
                            dve.sem_inc(alone, 1)
                            width = (qt + 1) * P
                            nc.vector.tensor_tensor_reduce(junk[:, qt, 0:width], PS[:, MAXB + at % MAXBANKS, 0:width],
                                                           mask[:, CH - width:CH], 1.0, LOWEST, ALU.add, ALU.max,
                                                           mpart[:, row, kc:kc + 1]).then_inc(ps_used, 1)
                    elif kind == "o_clear":
                        dve.wait_ge(pt_copied, NC * TPC + BASE)
                        nc.vector.memset(PS[:, OB, :], 0.0).then_inc(o_clear, 1)
                    elif kind == "neg_split":
                        dve.wait_ge(ps_used, passed_before(grp, piece_at(c, c, HG - 1, TPC - 1)) + 1)
                        hi, mid, lo = (mneg[:, a * HG * TPC:(a + 1) * HG * TPC] for a in range(PARTS))
                        link(nc.vector.tensor_reduce(mx[:, :], mpart[:, :, 0:c + 1], AX.X, ALU.max))
                        link(nc.vector.tensor_scalar(hi, mx[:, :], -1.0, None, ALU.mult))
                        link(nc.vector.scalar_tensor_tensor(out=mres[:, :], in0=mx[:, :], scalar=-1.0, in1=hi,
                                                            op0=ALU.mult, op1=ALU.subtract))
                        link(nc.vector.tensor_copy(mid, mres[:, :]))
                        nc.vector.tensor_tensor(lo, mres[:, :], mid, ALU.subtract).then_inc(neg_ready, 1)
                    elif kind == "neg_copy":
                        at, bank = neg_passage(grp, c)
                        dve.wait_ge(ps_ready, passed_before(grp, at) + 1)
                        dve.wait_ge(negs_loaded[c], 16 * grp + BASE)
                        nc.vector.tensor_copy(mT[0:PARTS * HG * TPC, c, :],
                                              PS[0:PARTS * HG * TPC, MAXB + bank, :].bitcast(bf16)[:, 0:P]
                                              ).then_inc(ps_used, 1)
                    elif kind == "vg":
                        copy_values(grp)
                    elif kind == "o_norm":
                        dve.wait_ge(o_turned, NC * grp + c + 1)
                        o = PS[:, OB, :].rearrange("p (j h v) -> p j h v", j=TPC, h=HG)
                        r = rec[:, :].rearrange("p (j h v) -> p j h v", j=TPC, h=HG)
                        link(nc.vector.reciprocal(r, o[:, :, :, D:VW]))
                        dst = AT[:, TPC * c:TPC * (c + 1), bass.ds(grp * HG * D, HG * D)]
                        nc.vector.tensor_tensor(dst.rearrange("p j (h d) -> p j h d", d=D), o[:, :, :, 0:D],
                                                r.broadcast_to([P, TPC, HG, D]), ALU.mult).then_inc(at_ready, 1)
                    elif kind == "a_copy":
                        a_copy(c)
                    elif kind == "y_stats":
                        y_stats(c)
                    elif kind == "x_stats":
                        x_stats(c)
                    elif kind == "x_norm":
                        x_norm(c)
                    elif kind == "x_copy":
                        x2_copy(c, MISC)

            def a_copy(c):
                dve.wait_ge(a_turned, c + 1)
                nc.vector.tensor_copy(aT[:, :], PS[:, MISC, :]).then_inc(aT_ready, 1)

            def y_stats(c):
                dve.wait_ge(proj_ready, c + 1)
                y = PS[:, MISC, :].rearrange("p (j f) -> p j f", j=TPC)
                bias = bo[:, :].unsqueeze(1).broadcast_to([P, TPC, C])
                nc.vector.tensor_tensor(yb[:, :, :], y, bias, ALU.add).then_inc(proj_used, 1)
                dve.wait_ge(proj_used, c + 1)
                norm_stats(lambda j: yb[:, j, :])

            def x_stats(c):
                dve.wait_ge(rstd_ready, 2 * c + 1)
                if c > 0:
                    dve.wait_ge(x2n_turned, c)
                for j in range(TPC):
                    last = normed(yn[:, j, :], yb[:, j, :], j)
                link(last)
                xc = X[:, TPC * c:TPC * (c + 1), :]
                link(nc.vector.tensor_tensor(xc, xc, yn[:, :, :], ALU.add))
                norm_stats(lambda j: X[:, TPC * c + j, :])

            def x_norm(c):
                dve.wait_ge(rstd_ready, 2 * c + 2)
                for j in range(TPC):
                    last = normed(yn[:, j, :], X[:, TPC * c + j, :], j)
                last.then_inc(x2n_ready, 1)

            def x2_copy(c, bank):
                dve.wait_ge(x2n_turned, c + 1)
                nc.vector.tensor_copy(X2T[:, c * CH:(c + 1) * CH], PS[:, bank, :]).then_inc(x2t_ready, 1)

            def copy_values(grp):
                if not (isinstance(grp, int) and grp == 0):
                    dve.wait_ge(pv_done, STEPS * grp)
                vg = VA[:, bass.ds(grp, 1), :, :, :].rearrange("p g t h v -> p (g t h v)")
                nc.vector.tensor_copy(VG[:, :, :, :].rearrange("p t h v -> p (t h v)"), vg).then_inc(vg_ready, 1)

            def links_in(items):
                return sum({"neg_split": 4, "o_norm": 1}.get(item[0], 0) for item in items)

            copy_values(0)
            first_links = count[0]
            before, per = first_links + links_in(START["dve"]), links_in(LOOP["dve"])
            stretch(0, START["dve"], first_links)
            with dve.Fori(0, G - 1) as g:
                stretch(g, LOOP["dve"], before + per * g)
            stretch(G - 1, END["dve"], before + per * (G - 1))

            def gated(c, m):
                dve.wait_ge(silu_done, FT * c + m + 1)
                nc.vector.scalar_tensor_tensor(out=hA[:, m, :], in0=PS[:, 2 * (m % 2) + 1, :],
                                               scalar=scales[:, 1, m:m + 1], in1=silu[:, m % 2, :],
                                               op0=ALU.mult, op1=ALU.mult).then_inc(up_used, 1)

            def out_stats(c):
                dve.wait_ge(y_ready, c + 1)
                nc.vector.tensor_tensor(yb[:, :, :], PS[:, 4:8, 0:C],
                                        s3[:, :].unsqueeze(1).broadcast_to([P, TPC, C]),
                                        ALU.mult).then_inc(y_used, 1)
                dve.wait_ge(y_used, c + 1 + BASE)
                norm_stats(lambda j: yb[:, j, :])

            def out(c):
                dve.wait_ge(rstd_ready, 2 * NC + c + 1)
                for j in range(TPC):
                    last = normed(yn[:, j, :], yb[:, j, :], j)
                link(last)
                dve.wait_ge(o_stored, 16 * c + BASE)
                nc.vector.tensor_tensor(ob[:, :, :], X[:, bass.ds(TPC * c, TPC), :], yn[:, :, :],
                                        ALU.add).then_inc(o_ready, 1)

            a_copy(NC - 1)
            gated(0, 0)
            y_stats(NC - 1)
            gated(0, 1)
            x_stats(NC - 1)
            gated(0, 2)
            gated(0, 3)
            x_norm(NC - 1)
            x2_copy(NC - 1, 0)
            out_stats(0)
            start, LINKS_M = base[0] + count[0], 3
            with dve.Fori(0, NC - 1) as last_c:
                base[0], count[0] = start + LINKS_M * last_c, 0
                c = last_c + 1
                gated(c, 0)
                gated(c, 1)
                out(last_c)
                gated(c, 2)
                gated(c, 3)
                out_stats(c)
                assert count[0] == LINKS_M
            base[0], count[0] = start + LINKS_M * (NC - 1), 0
            out(NC - 1)


def rope_tables():
    inv_freq = (1.0 / np.float32(ROPE_BASE) ** (np.arange(0, D, 2, dtype=np.float32) / D)).astype(np.float32)
    freqs = (np.arange(T, dtype=np.float32)[:, None] * inv_freq[None, :]).astype(np.float64)
    scale = 1.0 / np.sqrt(D)
    tables = np.stack([np.stack([f(freqs) * scale, f(freqs)], 1) for f in (np.cos, np.sin)], 1)
    tables = tables.reshape(T // P, P, 4 * D // 2).transpose(1, 0, 2)
    return np.ascontiguousarray(tables.reshape(P, -1), dtype=np.float32)


def kernel(L0_attn_x, L0_attn_Wq, L0_attn_bq, L0_attn_Wk, L0_attn_bk, L0_attn_Wv, L0_attn_bv, L0_attn_Wo,
           L0_attn_bo, L0_ffn_w1_w, L0_ffn_w1_s, L0_ffn_w2_w, L0_ffn_w2_s, L0_ffn_h1_w, L0_ffn_h1_s,
           L0_ffn_h2_w, L0_ffn_h2_s, L0_ffn_w3_w, L0_ffn_w3_s):
    import ml_dtypes
    import concourse.bacc as bacc
    from concourse.bass_utils import run_bass_kernel_spmd

    def lay(a):
        return np.ascontiguousarray(a)

    def columns(s):
        return np.asarray(s).reshape(FT, P).T

    tri = np.where(np.arange(P)[None, :] > np.arange(P)[:, None], np.float32(LOWEST), np.float32(0))
    arrays = {
        "x": lay(np.asarray(L0_attn_x).reshape(T, C)),
        "wqkv": lay(np.concatenate([np.asarray(w).T for w in (L0_attn_Wq, L0_attn_Wk, L0_attn_Wv)], 1)),
        "bqkv": lay(np.concatenate([np.asarray(b) for b in (L0_attn_bq, L0_attn_bk, L0_attn_bv)])[None, :]),
        "wo": lay(np.asarray(L0_attn_Wo).T),
        "bo": lay(np.asarray(L0_attn_bo)[None, :]),
        "w12": lay(np.concatenate([np.asarray(L0_ffn_w1_w).T, np.asarray(L0_ffn_w2_w).T], 1)),
        "h1": lay(np.asarray(L0_ffn_h1_w).T),
        "h2": lay(np.asarray(L0_ffn_h2_w).T),
        "w3": lay(np.asarray(L0_ffn_w3_w).T),
        "scales": lay(np.concatenate([columns(s) for s in (L0_ffn_w1_s, L0_ffn_w2_s, L0_ffn_h1_s,
                                                           L0_ffn_h2_s)], 1)),
        "s3": lay(np.asarray(L0_ffn_w3_s)[None, :]),
        "ident": np.eye(P, dtype=np.float32),
        "mask": lay(np.concatenate([np.zeros((P, CH - P), np.float32), tri], 1)),
        "rope": rope_tables(),
        "ones": np.ones((PARTS, COLS), ml_dtypes.bfloat16),
    }
    nc = bacc.Bacc("TRN2", target_bir_lowering=False, num_devices=1)
    args = [nc.dram_tensor(f"in_{n}", a.shape, mybir.dt.from_np(a.dtype), kind="ExternalInput").ap()
            for n, a in arrays.items()]
    out = nc.dram_tensor("out_y", (T, C), mybir.dt.float32, kind="ExternalOutput").ap()
    attention_mlp_kernel(nc, *args, out)
    r = run_bass_kernel_spmd(nc, [{f"in_{n}": a for n, a in arrays.items()}], core_ids=[0])
    return r.results[0]["out_y"].reshape(1, T, C)
```

```python
import numpy as np

import concourse.bass as bass
from concourse import mybir
from contextlib import ExitStack

T = 2048
C = 128
H = 16
D = C // H
P = 128
HG = 4
G = H // HG
CH = 512
NC = T // CH
TPC = CH // P
F = 512
FT = F // P
PARTS = 3
KR = PARTS * PARTS * D
VW = D + 1
EPS = 1e-5
LOWEST = -3.0e38
ROPE_BASE = 10000.0
COLS = NC * HG * CH
STEPS = sum(TPC * (c + 1) for c in range(NC))
FIRST_STEP = [sum(TPC * (b + 1) for b in range(c)) for c in range(NC)]
FIRST_PIECE = [sum(HG * TPC * (b + 1) for b in range(c)) for c in range(NC)]
PIECES = sum(HG * TPC * (c + 1) for c in range(NC))
RING = 4
SPLITS = 2 + 2 * FT
PAIRS = [(0, 0), (1, 0), (0, 1)]
NEG_AT = 2
RINGED = PIECES + NC
MAXBANKS = 3
BASE = 1

CUT_CHUNK = 2
LAG = 3
PACE = 24


def steps_of(dg, chunks):
    return [(dg, c, kt, max(0, kt - TPC * c) * P) for c in chunks for kt in range(TPC * (c + 1))]


def piece_at(c, kc, h, qt):
    n = (kc * HG + h) * TPC + qt
    return FIRST_PIECE[c] + c + n + (1 if n >= NEG_AT else 0)


def neg_at(c):
    return FIRST_PIECE[c + 1] + c + 1 + NEG_AT


def neg_passage(grp, c):
    if c < NC - 1:
        return neg_at(c), neg_at(c) % MAXBANKS
    return RINGED + (0 if isinstance(grp, int) and grp == G - 1 else NEG_AT), NEG_AT % MAXBANKS


def passed_before(grp, at):
    if isinstance(grp, int) and grp == 0 and at <= NEG_AT:
        return at
    return RINGED * grp + at - 1


CUT_AT = piece_at(NC - 1, 1, 0, 0)


def passages(dg, first, last):
    every = {piece_at(c, kc, h, qt): (dg, c, h, qt, kc) for c in range(NC) for kc in range(c + 1)
             for h in range(HG) for qt in range(TPC)}
    every.update({neg_at(c): (dg, c) for c in range(NC - 1)})
    every[NEG_AT] = (dg - 1, NC - 1)
    return [every[n] for n in range(first, min(last, RINGED))]


def order(carried, steps, ring, mlp_input=False):
    steps, in_loop = carried + steps, steps[-1][0] == 1
    pv_steps = steps if mlp_input else steps[:-LAG]
    hop = 0.22
    lists = {"pe": [], "act": [], "dve": [], "pool": [], "sp": []}
    t = {"pe": 0.0, "act": 0.0, "dve": 0.0}
    small, dve_due, sp_due = [], [], []
    exp_end, pv_end, used = {n: 0.0 for n in range(2 * len(carried))}, {}, []
    loaded, negated = {}, {}
    st, pv, at = HG * len(carried), 0, 0
    free = {"o": None if carried else 0.0, "vg": 0.0, "rows": 0.0}
    finished = [(0.0, c) for c in range(CUT_CHUNK - 1)] if mlp_input else []

    def on(engine, item, ready, cost):
        start = max(t[engine], ready)
        t[engine] = start + cost
        lists[engine].append(item)
        return t[engine]

    def dve_task(item, ready):
        kind, dg, c = item
        cost = {"o_norm": 0.5, "vg": 0.4, "a_copy": 0.6, "y_stats": 2.2, "x_stats": 3.2, "x_norm": 1.1,
                "x_copy": 1.3}[kind]
        end = on("dve", item, ready, cost)
        if kind == "vg":
            free["vg"] = end + hop
        elif kind == "o_norm":
            free["o"] = end + hop
            if c < NC - 1:
                finished.append((end + hop, c))
        elif kind == "a_copy":
            small.append((end + hop, ("a_proj", dg, c)))
        elif kind in ("y_stats", "x_stats"):
            lists["pool"].append(("rsqrt", dg, c, 0 if kind == "y_stats" else 1))
            dve_due.append((end + 1.7, ("x_stats" if kind == "y_stats" else "x_norm", dg, c)))
        elif kind == "x_norm":
            small.append((end + hop, ("x_turn", dg, c)))
        elif kind == "x_copy":
            free["rows"] = end + hop

    def dve_catch_up(now):
        while dve_due and min(dve_due)[0] <= max(now, t["dve"]):
            due = min(dve_due)
            dve_due.remove(due)
            dve_task(due[1], due[0])

    if in_loop:
        for c in range(CUT_CHUNK):
            sp_due.append((0.0, ("q", 1, c)))
            loaded["q", 1, c] = 3.0 * (c + 1)
        for c in range(NC):
            if piece_at(NC - 1, c, HG - 1, TPC - 1) < CUT_AT:
                sp_due.append((0.0, ("km", 1, c)))
                loaded["km", 1, c] = 9.0
    splits = list(range(2 + FT, SPLITS)) if mlp_input else []
    while True:
        dve_catch_up(t["pe"])
        if mlp_input and finished and free["rows"] is not None and at == len(ring):
            ready, c = finished.pop(0)
            small.append((max(ready, free["rows"], used[-1] + hop), ("a_turn", 0, c)))
            free["rows"] = None
        found = []
        if small:
            ready, item = min(small)
            found.append((ready, 0, "small", item))
        if at < len(ring):
            ready = used[at - MAXBANKS] + hop if at >= MAXBANKS else 0.0
            if len(ring[at]) == 2:
                found.append((max(ready, negated.get(ring[at], 0.0)), 1, "neg_turn", ring[at]))
            else:
                dg, c, h, qt, kc = ring[at]
                ready = max(ready, loaded.get(("q", dg, c), 0.0), loaded.get(("km", dg, kc), 0.0))
                ahead = at - (st - HG * len(carried))
                waiting = sum(u > t["pe"] for u in used[-MAXBANKS:])
                rank = 1 if (waiting < 1 and ahead < PACE) or ahead < PACE - 2 else 4
                found.append((ready, rank, "piece", ring[at]))
        if st < HG * len(steps):
            i, h = divmod(st, HG)
            if i < pv + RING:
                s = steps[i]
                ready = exp_end[st // 2 - 2] + hop if st >= HG else 0.0
                if s[2] == 0:
                    ready = max(ready, loaded.get(("neg", s[0], s[1]), 0.0), loaded.get(("ke", s[0], s[1]), 0.0))
                    if ("neg", s[0], s[1]) not in loaded and any(p[:2] == s[:2] for p in ring):
                        ready = None
                if ready is not None:
                    found.append((ready, 2 if t["act"] < t["pe"] + 2.0 else 3.5, "st", (s, h)))
        if pv < len(pv_steps) and 2 * pv + 1 in exp_end:
            s = pv_steps[pv]
            ready = exp_end[2 * pv + 1] + hop + (1.3 if s[2] >= TPC * s[1] else 0.0)
            if s[2] == 0:
                first = s[1] == 0
                if free["o"] is None or (first and free["vg"] is None):
                    ready = None
                else:
                    ready = max(ready, free["o"], free["vg"] if first else 0.0)
            if ready is not None:
                found.append((ready, 3, "pv", s))
        if not found:
            if not dve_due:
                break
            due = min(dve_due)
            dve_due.remove(due)
            dve_task(due[1], due[0])
            continue
        start, _, kind, item = min(found, key=lambda f: (max(f[0], t["pe"]), f[1]))
        if dve_due and min(dve_due)[0] < start and start > t["pe"]:
            t["pe"] = max(t["pe"], min(dve_due)[0])
            dve_catch_up(t["pe"])
            continue
        if kind == "small":
            small.remove(min(small))
            end = on("pe", item, start, 0.45)
            follow = {"o_turn": "o_norm", "a_turn": "a_copy", "a_proj": "y_stats", "x_turn": "x_copy"}[item[0]]
            dve_due.append((end + hop, (follow,) + item[1:]))
        elif kind == "neg_turn":
            at += 1
            end = on("pe", ("neg_turn",) + item, start, 0.06)
            used.append(on("dve", ("neg_copy",) + item, end + hop, 0.13))
            loaded[("neg",) + item] = used[-1] + 2.5
            sp_due.append((used[-1], ("neg",) + item))
        elif kind == "piece":
            dg, c, h, qt, kc = item
            at += 1
            width = CH if kc < c else (qt + 1) * P
            end = on("pe", ("piece",) + item, start, 0.003 + 0.213 * width / CH)
            used.append(on("dve", ("piece",) + item, end + hop, 0.07 + 0.00104 * width))
            if (h, qt) == (HG - 1, TPC - 1):
                if kc == c:
                    negated[dg, c] = on("dve", ("neg_split", dg, c), 0.0, 0.8) + hop
                if in_loop and dg == 0 and c == NC - 1:
                    sp_due.append((end, ("km", 1, kc)))
                    loaded["km", 1, kc] = end + 3.0
        elif kind == "st":
            s, h = item
            n = st // 2
            cols = CH - s[3]
            end = on("pe", ("st",) + s + (h,), start, 0.003 + 0.213 * cols / CH)
            st += 1
            if h % 2 == 1:
                slot_free = pv_end[n // 2 - RING] + hop if n // 2 >= RING else 0.0
                exp_end[n] = on("act", ("exp",) + s + (h // 2,), max(end + hop, slot_free),
                                0.05 + 0.00167 * cols)
            if h == HG - 1:
                dg, c, kt, _ = s
                if kt >= TPC * c:
                    lists["pool"].append(("mask",) + s)
                elif splits and at == len(ring) and kt % 2 == 0:
                    lists["pool"].append(("split", 0, splits.pop(0)))
                if kt == TPC * (c + 1) - 1 and c >= CUT_CHUNK:
                    sp_due.append((end, ("q", dg + 1, c)))
                    loaded["q", dg + 1, c] = end + 3.0
                if c == NC - 1 and kt % TPC == TPC - 1:
                    sp_due.append((end, ("ke", dg + 1, kt // TPC)))
                    loaded["ke", dg + 1, kt // TPC] = end + 3.0
        else:
            dg, c, kt, off = item
            pv_end[pv] = on("pe", ("pv",) + item, start, 0.06 + 0.00167 * (CH - off))
            if kt == 0:
                free["o"] = None
            if kt == TPC * (c + 1) - 1:
                done = on("act", ("o_copy", dg, c), pv_end[pv] + hop, 0.5)
                small.append((done + hop, ("o_turn", dg, c)))
                if c == NC - 1 and not mlp_input:
                    free["vg"] = None
                    dve_due.append((pv_end[pv] + hop, ("vg", dg + 1, 0)))
            pv += 1
    lists["sp"] = [item for _, item in sorted(sp_due)]
    return lists


FIRST_HALF = steps_of(0, range(CUT_CHUNK))
START = order([], FIRST_HALF, [e for e in passages(0, 0, CUT_AT) if e[0] == 0])
for tile in range(TPC):
    START["pe"].insert(MAXBANKS + 3 * tile, ("parts_turn", 0, tile))
START["dve"].insert(START["dve"].index(("neg_split", 0, 0)) + 1, ("o_clear", 0, 0))
LOOP = order(FIRST_HALF[-LAG:], steps_of(0, range(CUT_CHUNK, NC)) + steps_of(1, range(CUT_CHUNK)),
             passages(0, CUT_AT, RINGED) + passages(1, 0, CUT_AT))
END = order(FIRST_HALF[-LAG:], steps_of(0, range(CUT_CHUNK, NC)), passages(0, CUT_AT, RINGED)
            + [(0, NC - 1)], True)
END["pe"].insert(END["pe"].index(("o_turn", 0, NC - 1)) - 1, ("up", 0, 0))
END["pe"].insert(END["pe"].index(("o_turn", 0, NC - 1)), ("up", 0, 1))
END["pe"].remove(("x_turn", 0, NC - 2))
END["dve"].remove(("x_copy", 0, NC - 2))
END["dve"].remove(("x_norm", 0, NC - 2))
END["dve"].remove(("x_stats", 0, NC - 2))
place = END["dve"].index(("o_norm", 0, NC - 1))
END["dve"][place:place + 1] = [("x_stats", 0, NC - 2), ("o_norm", 0, NC - 1), ("gated", 0, 0)]


def attention_mlp_kernel(nc, x_in, wqkv_in, bqkv_in, wo_in, bo_in, w12_in, h1_in, h2_in, w3_in,
                         scales_in, s3_in, ident_in, mask_in, rope_in, ones_in, out_dram):
    f32, bf16, f32r = mybir.dt.float32, mybir.dt.bfloat16, mybir.dt.float32r
    ALU, ACT, AX = mybir.AluOpType, mybir.ActivationFunctionType, mybir.AxisListType

    parts_dram = nc.dram_tensor("parts_dram", [2, NC, PARTS, D, H * CH], bf16, kind="Internal").ap()

    ctx = ExitStack()
    with ctx:
        def sb(name, shape, dt=f32, within=ctx):
            return within.enter_context(nc.sbuf_tensor(name, shape, dt))

        def sem(name):
            return ctx.enter_context(nc.semaphore(name))

        VA = sb("VA", [P, G, T // P, HG, VW])
        VG = sb("VG", [P, T // P, HG, VW])
        X = sb("X", [P, T // P, C])
        AT = sb("AT", [P, T // P, C])
        OT = sb("OT", [P, CH])
        work = sb("work", [P, 5632])
        XN = sb("XN", [P, TPC, C])
        XT = sb("XT", [P, CH])
        wqkv = sb("wqkv", [P, 3 * C])
        bqkv = sb("bqkv", [P, 3 * C])
        wo = sb("wo", [P, C])
        bo = sb("bo", [P, C])
        s3 = sb("s3", [P, C])
        scales = sb("scales", [P, 4, FT])
        ident = sb("ident", [P, P])
        identb = sb("identb", [P, P], bf16)
        mask = sb("mask", [P, CH])
        rope = sb("rope", [P, T // P, 2, 2, D // 2])
        junk = sb("junk", [P, 4, CH], bf16)
        mpart = sb("mpart", [P, HG * TPC, NC])
        mx = sb("mx", [P, HG * TPC])
        mres = sb("mres", [P, HG * TPC])
        mneg = sb("mneg", [P, P], bf16)
        mT = sb("mT", [P, NC, P], bf16)
        rec = sb("rec", [P, TPC * HG])
        stats = sb("stats", [P, TPC, 6])
        mv = sb("mv", [P, TPC, 2])
        var = sb("var", [P, TPC])
        rstd = sb("rstd", [P, TPC])
        nhalf = sb("nhalf", [P, TPC])
        yb = sb("yb", [P, TPC, C])
        yn = sb("yn", [P, TPC, C])
        ob = sb("ob", [P, TPC, C])
        silu = sb("silu", [P, 2, CH])
        aT = sb("aT", [P, CH])

        w12_high = sb("w12_high", [P, 2, F], f32r)
        h1_parts = [sb(f"h1_{n}", [P, FT, F], f32r) for n in ("high", "low")]
        X2T_high = sb("X2T_high", [P, T], f32r)

        early = ctx.enter_context(ExitStack())
        pieces3 = sb("pieces3", [P, TPC, PARTS, 2 * C], bf16, early)
        piecesT = sb("piecesT", [P, 2 * PARTS, CH], bf16, early)
        early.close()
        X2T_low = sb("X2T_low", [P, T], f32r)
        w12_parts = [w12_high, sb("w12_low", [P, 2, F], f32r)]

        attention = ctx.enter_context(ExitStack())
        KM = sb("KM", [P, COLS], bf16, attention)
        PR = sb("PR", [P, RING, HG, CH], f32, attention)
        QA = sb("QA", [P, COLS], bf16, attention)
        KE = sb("KE", [P, COLS], bf16, attention)
        attention.close()
        h2_parts = [sb(f"h2_{n}", [P, FT, F], f32r) for n in ("high", "low")]
        hA_parts = [sb(f"hA_{n}", [P, FT, CH], f32r) for n in ("high", "low")]
        hB_parts = [sb(f"hB_{n}", [P, FT, CH], f32r) for n in ("high", "low")]
        hC = sb("hC", [P, FT, CH])
        whole = sb("whole", [P, 4, CH])

        def tile2(at):
            return work[:, at:at + TPC * 2 * C].rearrange("p (j n) -> p j n", j=TPC)

        qk, ra, rb, qr, qres = (tile2(n * TPC * 2 * C) for n in range(5))
        at = 5 * TPC * 2 * C
        xstats = work[:, at:at + 6 * T // P].rearrange("p (t n) -> p t n", n=6)
        xmv = work[:, at + 6 * T // P:at + 8 * T // P].rearrange("p (t n) -> p t n", n=2)
        xvar = work[:, at + 8 * T // P:at + 9 * T // P]
        xrstd = work[:, at + 9 * T // P:at + 10 * T // P]
        xhalf = work[:, at + 10 * T // P:at + 11 * T // P]
        w12 = work[:, 0:2 * F].rearrange("p (a n) -> p a n", a=2)
        h1 = work[:, 2 * F:2 * F + FT * F].rearrange("p (k n) -> p k n", k=FT)
        h2 = work[:, 2 * F + FT * F:2 * F + 2 * FT * F].rearrange("p (k n) -> p k n", k=FT)
        w3 = work[:, 2 * F + 2 * FT * F:].rearrange("p (k n) -> p k n", k=FT)

        PS = ctx.enter_context(nc.psum_tensor("PS", [P, 8, CH], f32))
        MAXB, OB, MISC = 4, 7, 6

        def parts_bank(c, j):
            first = 0 if isinstance(c, int) and c == NC - 1 else MISC
            return PS[:, first if j % 2 == 0 else OB, :].bitcast(bf16)[:, 0:2 * PARTS * P]

        x0_loaded = sem("x0_loaded")
        x_loaded, w_loaded, c_loaded = sem("x_loaded"), sem("w_loaded"), sem("c_loaded")
        idb_ready = sem("idb_ready")
        ke_padded = sem("ke_padded")
        q_padded, k_padded = sem("q_padded"), sem("k_padded")
        xvar_ready, xrstd_ready = sem("xvar_ready"), sem("xrstd_ready")
        var_ready, rstd_ready, xn_ready = sem("var_ready"), sem("rstd_ready"), sem("xn_ready")
        xn_turned, xt_ready, qkv_ready = sem("xn_turned"), sem("xt_ready"), sem("qkv_ready")
        qk_ready, ra_ready, qr_ready = sem("qk_ready"), sem("ra_ready"), sem("qr_ready")
        rb_ready = sem("rb_ready")
        hi_ready, res_ready, mid_ready = sem("hi_ready"), sem("res_ready"), sem("mid_ready")
        lo_ready, pt_turned, pt_copied = sem("lo_ready"), sem("pt_turned"), sem("pt_copied")
        pt_stored = sem("pt_stored")
        nh_ready = sem("nh_ready")
        q_loaded = [sem(f"q_loaded{c}") for c in range(NC)]
        km_loaded = [sem(f"km_loaded{c}") for c in range(NC)]
        ke_loaded = [sem(f"ke_loaded{c}") for c in range(NC)]
        negs_loaded = [sem(f"negs_loaded{c}") for c in range(NC)]
        ones_loaded = sem("ones_loaded")
        ps_ready, ps_used = sem("piece_ready"), sem("piece_used")
        neg_ready = sem("neg_ready")
        o_clear = sem("o_clear")
        st_ready, exp_done, masked = sem("scores_ready"), sem("exp_done"), sem("masked")
        vg_ready, pv_done = sem("vg_ready"), sem("pv_done")
        o_copied, o_turned = sem("o_copied"), sem("o_turned")
        at_ready, a_turned, aT_ready = sem("at_ready"), sem("a_turned"), sem("aT_ready")
        proj_ready, proj_used = sem("proj_ready"), sem("proj_used")
        x2n_ready, x2n_turned = sem("x2n_ready"), sem("x2n_turned")
        x2t_ready = sem("x2t_ready")
        mlp_loaded, w_split = sem("mlp_loaded"), sem("w_split")
        w_high = sem("w_high")
        hA_high, hA_low = sem("hA_high"), sem("hA_low")
        hB_whole = sem("hB_whole")
        hB_high, hB_low = sem("hB_high"), sem("hB_low")
        up_ready, silu_done, up_used = sem("up_ready"), sem("silu_done"), sem("up_used")
        g1_in, g2_in, g2_done = sem("g1_in"), sem("g2_in"), sem("g2_done")
        y_ready, y_used, o_ready, o_stored = sem("y_ready"), sem("y_used"), sem("o_ready"), sem("o_stored")
        vstep = sem("vstep")

        alone = sem("alone")
        from_base = [xn_turned, qk_ready, pt_copied, qkv_ready, pt_turned, pt_stored, lo_ready, y_used,
                     g2_done, up_used, o_stored] + negs_loaded

        block = ctx.enter_context(nc.Block())

        @block.sync
        def _(sp):
            for s in from_base:
                sp.sem_inc(s, BASE)
            x_tiles = x_in.rearrange("(t p) f -> p t f", p=P)
            sp.dma_start(X[:, 0:TPC, :], x_tiles[:, 0:TPC, :]).then_inc(x0_loaded, 16)
            sp.dma_start(ident[:, :], ident_in).then_inc(w_loaded, 16)
            sp.dma_start(wqkv[:, :], wqkv_in).then_inc(w_loaded, 16)
            sp.dma_start(bqkv[:, :], bqkv_in.broadcast_to([P, 3 * C])).then_inc(w_loaded, 16)
            sp.dma_start(X[:, TPC:T // P, :], x_tiles[:, TPC:T // P, :]).then_inc(x_loaded, 16)
            sp.dma_start(rope[:, :, :, :, :].rearrange("p t a b f -> p (t a b f)"), rope_in).then_inc(w_loaded, 16)
            sp.dma_start(mask[:, :], mask_in).then_inc(c_loaded, 16)
            sp.dma_start(wo[:, :], wo_in).then_inc(c_loaded, 16)
            sp.dma_start(bo[:, :], bo_in.broadcast_to([P, C])).then_inc(c_loaded, 16)
            sp.dma_start(s3[:, :], s3_in.broadcast_to([P, C])).then_inc(c_loaded, 16)
            sp.dma_start(scales[:, :, :].rearrange("p a m -> p (a m)"), scales_in).then_inc(c_loaded, 16)
            sp.wait_ge(q_padded, 1)
            sp.wait_ge(k_padded, 2)
            sp.wait_ge(ke_padded, 2)
            sp.dma_start(KE[KR:KR + PARTS, :], ones_in).then_inc(ones_loaded, 16)

            def load_q(g, c):
                for a in range(PARTS):
                    q = parts_dram[0, c, a, :, bass.ds(g * HG * CH, HG * CH)]
                    sp.dma_start(QA[a * PARTS * D:(a + 1) * PARTS * D, c * HG * CH:(c + 1) * HG * CH],
                                 q.unsqueeze(0).broadcast_to([PARTS, D, HG * CH])).then_inc(q_loaded[c], 16)

            def load_k(dst, loaded, g, c):
                k = parts_dram[1, c, :, :, bass.ds(g * HG * CH, HG * CH)].rearrange("a d s -> (a d) s")
                rows = dst[0:KR, c * HG * CH:(c + 1) * HG * CH]
                sp.dma_start(rows,
                             k.unsqueeze(0).broadcast_to([PARTS, PARTS * D, HG * CH])).then_inc(loaded[c], 16)

            def load_negs(g, c):
                sp.wait_ge(ps_used, passed_before(g, neg_passage(g, c)[0]) + 1)
                sp.sem_inc(alone, 1)
                rows = QA[KR:KR + PARTS, c * HG * CH:(c + 1) * HG * CH]
                sp.dma_start(rows.rearrange("p (a s) -> p a s", s=P),
                             mT[0:PARTS * HG * TPC, c, :]).then_inc(negs_loaded[c], 16)

            for c in range(NC):
                sp.wait_ge(pt_copied, TPC * (c + 1) + BASE)
                for i in range(2 * PARTS):
                    sp.dma_start(parts_dram[i // PARTS, c, i % PARTS].rearrange("d (h s) -> h d s", h=H),
                                 piecesT[:, i, :]).then_inc(pt_stored, 16)
                if c == NC - 1:
                    load_negs(0, 0)
                sp.wait_ge(pt_stored, 96 * (c + 1) + BASE)
                load_q(0, c)
                load_k(KM, km_loaded, 0, c)
                load_k(KE, ke_loaded, 0, c)
            def stretch(g, items):
                for kind, dg, c in items:
                    if kind == "neg":
                        load_negs(g + dg, c)
                    elif kind == "q":
                        sp.wait_ge(st_ready, 2 * (STEPS * (g + dg - 1) + FIRST_STEP[c] + TPC * (c + 1)))
                        sp.sem_inc(alone, 1)
                        load_q(g + dg, c)
                    elif kind == "ke":
                        sp.wait_ge(st_ready, 2 * (STEPS * (g + dg - 1) + FIRST_STEP[NC - 1] + TPC * (c + 1)))
                        sp.sem_inc(alone, 1)
                        load_k(KE, ke_loaded, g + dg, c)
                    elif kind == "km":
                        last = passed_before(g + dg - 1, piece_at(NC - 1, c, HG - 1, TPC - 1))
                        sp.wait_ge(ps_ready, last + 1)
                        sp.sem_inc(alone, 1)
                        load_k(KM, km_loaded, g + dg, c)

            stretch(0, [item for item in START["sp"] if item != ("neg", 0, 0)])
            sp.dma_start(w12[:, :, :].rearrange("p a n -> p (a n)"), w12_in).then_inc(mlp_loaded, 16)
            sp.dma_start(h1, h1_in.rearrange("(k p) n -> p k n", p=P)).then_inc(mlp_loaded, 16)
            sp.dma_start(h2, h2_in.rearrange("(k p) n -> p k n", p=P)).then_inc(mlp_loaded, 16)
            sp.dma_start(w3, w3_in.rearrange("(k p) n -> p k n", p=P)).then_inc(mlp_loaded, 16)
            with sp.Fori(0, G - 1) as g:
                stretch(g, LOOP["sp"])
            stretch(G - 1, [item for item in END["sp"] if item[0] == "neg"])
            with sp.Fori(0, NC) as c:
                sp.wait_ge(o_ready, c + 1)
                sp.dma_start(out_dram[bass.ds(c * CH, CH), :].rearrange("(j p) f -> p j f", p=P),
                             ob[:, :, :]).then_inc(o_stored, 16)
            sp.wait_ge(o_stored, 16 * NC + BASE)

        @block.tensor
        def _(pe):
            pe.wait_ge(w_loaded, 64)

            def x_turn(c):
                pe.wait_ge(xn_ready, c + 1)
                for j in range(TPC):
                    last = nc.tensor.transpose(PS[:, MAXB, j * P:(j + 1) * P], XN[:, j, :], ident[:, :])
                last.then_inc(xn_turned, 1)

            def qkv(c):
                pe.wait_ge(xt_ready, c + 1)
                for j in range(TPC):
                    if not isinstance(c, int):
                        pe.wait_ge(qk_ready, TPC * (c - 1) + j + 1 + BASE)
                    nc.tensor.matmul(PS[:, j, 0:3 * C], XT[:, j * P:(j + 1) * P], wqkv[:, :],
                                     start=True, stop=True).then_inc(qkv_ready, 1)

            def parts_turn(c, j):
                pe.wait_ge(lo_ready, TPC * c + j + 1 + BASE)
                if j >= 2:
                    pe.wait_ge(pt_copied, TPC * c + j - 1 + BASE)
                else:
                    pe.wait_ge(pt_copied, TPC * c + BASE)
                for i in range(2 * PARTS):
                    a = i // PARTS
                    last = nc.tensor.transpose(parts_bank(c, j)[:, i * P:(i + 1) * P],
                                               pieces3[:, j, i % PARTS, a * C:(a + 1) * C], identb[:, :])
                last.then_inc(pt_turned, 1)

            x_turn(0)
            qkv(0)
            pe.wait_ge(idb_ready, 1)
            with pe.Fori(0, NC - 1) as c:
                x_turn(c + 1)
                qkv(c + 1)
                for j in range(TPC):
                    parts_turn(c, j)

            def up(c, m):
                if m >= 2:
                    pe.wait_ge(up_used, FT * c + m - 1 + BASE)
                else:
                    pe.wait_ge(g2_done, FT * c + BASE)
                cols = bass.ds(c * CH, CH)
                for a in range(2):
                    for n, (w, x) in enumerate(PAIRS):
                        last = nc.tensor.matmul(PS[:, 2 * (m % 2) + a, :], w12_parts[w][:, a, m * P:(m + 1) * P],
                                                (X2T_high, X2T_low)[x][:, cols], start=(n == 0),
                                                stop=(n == len(PAIRS) - 1))
                last.then_inc(up_ready, 1)

            def ring_free(grp, at):
                if at >= MAXBANKS:
                    pe.wait_ge(ps_used, passed_before(grp, at - MAXBANKS) + 1)
                elif not (isinstance(grp, int) and grp == 0):
                    pe.wait_ge(ps_used, passed_before(grp, 0))

            def stretch(g, items):
                for item in items:
                    kind, c = item[0], item[2]
                    grp = g + item[1]
                    if kind == "parts_turn":
                        parts_turn(NC - 1, c)
                    elif kind == "piece":
                        _, _, _, h, qt, kc = item
                        at = piece_at(c, kc, h, qt)
                        if (h, qt, kc) == (0, 0, 0):
                            pe.wait_ge(q_loaded[c], 16 * PARTS * (grp + 1))
                        if (h, qt, kc) == (0, 0, c):
                            pe.wait_ge(km_loaded[c], 16 * (grp + 1))
                        ring_free(grp, at)
                        width = CH if kc < c else (qt + 1) * P
                        q0, k0 = (c * HG + h) * CH + qt * P, (kc * HG + h) * CH
                        nc.tensor.matmul(PS[:, MAXB + at % MAXBANKS, 0:width], QA[:, q0:q0 + P],
                                         KM[:, k0:k0 + width], start=True, stop=True).then_inc(ps_ready, 1)
                    elif kind == "neg_turn":
                        pe.wait_ge(neg_ready, NC * grp + c + 1)
                        at, bank = neg_passage(grp, c)
                        ring_free(grp, at)
                        pe.sem_inc(alone, 1)
                        nc.tensor.transpose(PS[:, MAXB + bank, :].bitcast(bf16)[:, 0:P],
                                            mneg[:, :], identb[:, :]).then_inc(ps_ready, 1)
                    elif kind == "st":
                        _, _, _, kt, off, h = item
                        if kt == 0 and h == 0:
                            pe.wait_ge(negs_loaded[c], 16 * (grp + 1) + BASE)
                            pe.wait_ge(ke_loaded[c], 16 * (grp + 1))
                            if c == 0:
                                pe.wait_ge(ones_loaded, 16)
                        n = 2 * (FIRST_STEP[c] + kt) + h // 2
                        if h % 2 == 0 and not (isinstance(grp, int) and grp == 0 and n < 2):
                            pe.wait_ge(exp_done, 2 * STEPS * grp + n - 1)
                        k0 = (kt // TPC * HG + h) * CH + kt % TPC * P
                        q0 = (c * HG + h) * CH + off
                        last = nc.tensor.matmul(PS[:, h, off:CH], KE[:, k0:k0 + P],
                                                QA[:, q0:q0 + CH - off], start=True, stop=True)
                        if h % 2 == 1:
                            last.then_inc(st_ready, 1)
                    elif kind == "pv":
                        _, _, _, kt, off = item
                        step = FIRST_STEP[c] + kt
                        if kt >= TPC * c:
                            pe.wait_ge(masked, NC * TPC * grp + TPC * c + kt - TPC * c + 1)
                        else:
                            pe.wait_ge(exp_done, 2 * (STEPS * grp + step + 1))
                        if kt == 0 and c == 0:
                            pe.wait_ge(vg_ready, grp + 1)
                            pe.wait_ge(o_clear, 1)
                        if kt == 0 and not (isinstance(grp, int) and grp == 0 and c == 0):
                            pe.wait_ge(at_ready, NC * grp + c)
                        for h in range(HG):
                            last = nc.tensor.matmul(PS[32 * h:32 * h + VW, OB, off:CH], VG[:, kt, h, :],
                                                    PR[:, step % RING, h, off:CH], start=(kt == 0),
                                                    stop=(kt == TPC * (c + 1) - 1))
                        last.then_inc(pv_done, 1)
                    elif kind == "o_turn":
                        pe.wait_ge(o_copied, NC * grp + c + 1)
                        for j in range(TPC):
                            last = nc.tensor.transpose(PS[:, OB, j * P:(j + 1) * P],
                                                       OT[:, j * P:(j + 1) * P], ident[:, :])
                        last.then_inc(o_turned, 1)
                    elif kind == "up":
                        if c == 0:
                            pe.wait_ge(exp_done, 2 * STEPS * G)
                            pe.wait_ge(w_split, SPLITS)
                            pe.wait_ge(x2t_ready, 1)
                        up(0, c)
                    elif kind == "a_turn":
                        if c == 0:
                            pe.wait_ge(ps_used, passed_before(G - 1, RINGED) + 1)
                        else:
                            pe.wait_ge(x2t_ready, c)
                        a_turn(c, MISC)
                    elif kind == "a_proj":
                        a_proj(c, MISC)
                    elif kind == "x_turn":
                        x2_turn(c, MISC)

            def a_turn(c, bank):
                pe.wait_ge(at_ready, NC * (G - 1) + c + 1)
                for j in range(TPC):
                    last = nc.tensor.transpose(PS[:, bank, j * P:(j + 1) * P], AT[:, TPC * c + j, :], ident[:, :])
                last.then_inc(a_turned, 1)

            def a_proj(c, bank):
                pe.wait_ge(aT_ready, c + 1)
                pe.wait_ge(c_loaded, 80)
                for j in range(TPC):
                    last = nc.tensor.matmul(PS[:, bank, j * P:(j + 1) * P], aT[:, j * P:(j + 1) * P],
                                            wo[:, :], start=True, stop=True)
                last.then_inc(proj_ready, 1)

            def x2_turn(c, bank):
                pe.wait_ge(x2n_ready, c + 1)
                for j in range(TPC):
                    last = nc.tensor.transpose(PS[:, bank, j * P:(j + 1) * P], yn[:, j, :], ident[:, :])
                last.then_inc(x2n_turned, 1)

            stretch(0, START["pe"])
            with pe.Fori(0, G - 1) as g:
                stretch(g, LOOP["pe"])
            stretch(G - 1, END["pe"])

            def hidden(c, k, weights, inputs, banks, low_ready, done):
                last_k = k == FT - 1
                products = [(n, m) for n in range(len(PAIRS)) for m in range(FT)]
                if last_k:
                    products.sort(key=lambda p: p[1])
                waited = False
                for n, m in products:
                    w, x = PAIRS[n]
                    if x == 1 and not waited:
                        pe.wait_ge(low_ready, FT * c + k + 1)
                        waited = True
                    ins = nc.tensor.matmul(PS[:, banks + m, :], weights[w][:, k, m * P:(m + 1) * P],
                                           inputs[x][:, k, :], start=(k == 0 and n == 0),
                                           stop=(last_k and n == len(PAIRS) - 1))
                    if last_k and n == len(PAIRS) - 1:
                        ins.then_inc(done, 1)

            def hidden1(c, k):
                pe.wait_ge(hA_high, FT * c + k + 1)
                hidden(c, k, h1_parts, hA_parts, 4, hA_low, g1_in)

            def hidden2_down(c):
                for k in range(FT):
                    pe.wait_ge(hB_high, FT * c + k + 1)
                    hidden(c, k, h2_parts, hB_parts, 0, hB_low, g2_in)
                for k in range(FT):
                    pe.wait_ge(g2_done, FT * c + k + 1 + BASE)
                    for j in range(TPC):
                        last = nc.tensor.matmul(PS[:, 4 + j, 0:C], hC[:, k, j * P:(j + 1) * P], w3[:, k, :],
                                                start=(k == 0), stop=(k == FT - 1))
                last.then_inc(y_ready, 1)

            a_turn(NC - 1, OB)
            up(0, 2)
            x2_turn(NC - 2, MISC)
            a_proj(NC - 1, OB)
            up(0, 3)
            pe.wait_ge(proj_used, NC)
            pe.wait_ge(x2t_ready, NC - 1)
            for k in range(FT):
                hidden1(0, k)
                if k == FT - 2:
                    pe.wait_ge(up_used, FT + BASE)
                    x2_turn(NC - 1, 0)
            pe.wait_ge(x2t_ready, NC)
            pe.wait_ge(mlp_loaded, 64)
            hidden2_down(0)
            with pe.Fori(0, NC - 1) as last_c:
                c = last_c + 1
                for m in range(FT):
                    up(c, m)
                pe.wait_ge(y_used, c + BASE)
                for k in range(FT):
                    hidden1(c, k)
                hidden2_down(c)

        @block.scalar
        def _(act):
            def x_copy(c):
                act.wait_ge(xn_turned, c + 1 + BASE)
                if not isinstance(c, int):
                    act.wait_ge(qkv_ready, TPC * c + BASE)
                nc.scalar.activation(XT[:, :], PS[:, MAXB, :], ACT.Copy).then_inc(xt_ready, 1)

            def parts(c):
                act.wait_ge(pt_turned, TPC * c + BASE)
                for j in range(TPC):
                    act.wait_ge(qr_ready, TPC * c + j + 1)
                    nc.scalar.activation(pieces3[:, j, 0, :], qr[:, j, :], ACT.Copy).then_inc(hi_ready, 1)
                for j in range(TPC):
                    act.wait_ge(res_ready, TPC * c + j + 1)
                    nc.scalar.activation(pieces3[:, j, 1, :], qres[:, j, :], ACT.Copy).then_inc(mid_ready, 1)
                act.wait_ge(pt_stored, 96 * c + BASE)
                for j in range(TPC):
                    act.wait_ge(pt_turned, TPC * c + j + 1 + BASE)
                    nc.scalar.activation(piecesT[:, :, j * P:(j + 1) * P],
                                         parts_bank(c, j).rearrange("p (i s) -> p i s", s=P),
                                         ACT.Copy).then_inc(pt_copied, 1)

            act.wait_ge(k_padded, 1)
            for n in range(2):
                nc.scalar.activation(KE[P // 2:P, n * COLS // 2:(n + 1) * COLS // 2], KM[P // 2:P, 0:COLS // 2],
                                     ACT.Copy).then_inc(ke_padded, 1)
            x_copy(0)
            with act.Fori(0, NC - 1) as c:
                x_copy(c + 1)
                parts(c)
            parts(NC - 1)

            def stretch(g, items):
                for item in items:
                    c, grp = item[2], g + item[1]
                    if item[0] == "exp":
                        _, _, _, kt, off, pr = item
                        step = FIRST_STEP[c] + kt
                        if pr == 0 and not (isinstance(grp, int) and grp == 0 and step < RING):
                            act.wait_ge(pv_done, STEPS * grp + step - RING + 1)
                        act.wait_ge(st_ready, 2 * (STEPS * grp + step) + pr + 1)
                        nc.scalar.activation(PR[:, step % RING, 2 * pr:2 * pr + 2, off:CH],
                                             PS[:, 2 * pr:2 * pr + 2, off:CH], ACT.Exp).then_inc(exp_done, 1)
                    else:
                        act.wait_ge(pv_done, STEPS * grp + FIRST_STEP[c] + TPC * (c + 1))
                        if not (isinstance(grp, int) and grp == 0 and c == 0):
                            act.wait_ge(o_turned, NC * grp + c)
                        nc.scalar.activation(OT[:, :], PS[:, OB, :], ACT.Copy).then_inc(o_copied, 1)

            stretch(0, START["act"])
            with act.Fori(0, G - 1) as g:
                stretch(g, LOOP["act"])
            stretch(G - 1, END["act"])

            with act.Fori(0, NC) as c:
                for step in range(FT + 1):
                    m = step
                    if m < FT:
                        act.wait_ge(up_ready, FT * c + m + 1)
                        if m >= 2:
                            act.wait_ge(up_used, FT * c + m - 1 + BASE)
                        else:
                            act.wait_ge(up_used, FT * c + BASE)
                        nc.scalar.activation(silu[:, m % 2, :], PS[:, 2 * (m % 2), :], ACT.Silu,
                                             scale=scales[:, 0, m:m + 1]).then_inc(silu_done, 1)
                    m = step - 1
                    if m >= 0:
                        act.wait_ge(up_used, FT * c + m + 1 + BASE)
                        nc.scalar.activation(hA_parts[0][:, m, :], whole[:, m, :], ACT.Copy).then_inc(hA_high, 1)
                for m in range(FT):
                    act.wait_ge(g1_in, FT * c + m + 1)
                    if m == 0:
                        act.wait_ge(hA_low, FT * (c + 1))
                    for dst, done in ((hB_parts[0], hB_high), (whole, hB_whole)):
                        nc.scalar.activation(dst[:, m, :], PS[:, 4 + m, :], ACT.Gelu,
                                             scale=scales[:, 2, m:m + 1]).then_inc(done, 1)
                for m in range(FT):
                    act.wait_ge(g2_in, FT * c + m + 1)
                    nc.scalar.activation(hC[:, m, :], PS[:, m, :], ACT.Gelu,
                                         scale=scales[:, 3, m:m + 1]).then_inc(g2_done, 1)

        @block.gpsimd
        def _(pool):
            nc.gpsimd.memset(nhalf[:, :], -0.5)
            nc.gpsimd.memset(xhalf, -0.5).then_inc(nh_ready, 1)
            pool.wait_ge(nh_ready, 1)
            for n in range(2):
                nc.gpsimd.memset(KM[P // 2:P, n * COLS // 2:(n + 1) * COLS // 2], 0.0).then_inc(k_padded, 1)
                pool.wait_ge(k_padded, n + 1)
            pool.wait_ge(w_loaded, 64)

            def rsqrt(n):
                pool.wait_ge(var_ready, n)
                nc.gpsimd.tensor_tensor(rstd[:, :], var[:, :], nhalf[:, :], ALU.pow).then_inc(rstd_ready, 1)

            def turned(c):
                for j in range(TPC):
                    pool.wait_ge(qk_ready, TPC * c + j + 1 + BASE)
                    cos = rope[:, bass.ds(TPC * c + j, 1), 0, :, :].rearrange("p t b f -> p (t b) f")
                    nc.gpsimd.tensor_tensor(
                        ra[:, j, :].rearrange("p (b h f) -> p b h f", b=2, f=D // 2),
                        qk[:, j, :].rearrange("p (b h f) -> p b h f", b=2, f=D // 2),
                        cos.unsqueeze(2).broadcast_to([P, 2, 2 * H, D // 2]), ALU.mult).then_inc(ra_ready, 1)

            def low_parts(c):
                for j in range(TPC):
                    pool.wait_ge(mid_ready, TPC * c + j + 1)
                    nc.gpsimd.tensor_tensor(pieces3[:, j, 2, :], qres[:, j, :], pieces3[:, j, 1, :],
                                            ALU.subtract).then_inc(lo_ready, 1)

            for c in range(NC):
                pool.wait_ge(xvar_ready, c + 1)
                tiles = slice(TPC * c, TPC * (c + 1))
                nc.gpsimd.tensor_tensor(xrstd[:, tiles], xvar[:, tiles], xhalf[:, tiles],
                                        ALU.pow).then_inc(xrstd_ready, 1)
            with pool.Fori(0, NC) as c:
                turned(c)
                low_parts(c)

            def stretch(g, items):
                for item in items:
                    c, grp = item[2], g + item[1]
                    if item[0] == "rsqrt":
                        rsqrt(2 * c + item[3] + 1)
                    elif item[0] == "split":
                        if c == 2 + FT:
                            pool.wait_ge(ps_ready, passed_before(G - 1, RINGED) + 1)
                        split(c)
                    else:
                        _, _, _, kt, off = item
                        step = FIRST_STEP[c] + kt
                        pool.wait_ge(exp_done, 2 * (STEPS * grp + step + 1))
                        pool.sem_inc(alone, 1)
                        diag = PR[:, step % RING, :, off:off + P]
                        nc.gpsimd.affine_select(out=diag, in_=diag, compare_op=ALU.is_ge, fill=0.0, base=0,
                                                pattern=[[0, HG], [1, P]],
                                                channel_multiplier=-1).then_inc(masked, 1)

            def split(n):
                parts, k = ((w12_parts, n) if n < 2 else (h1_parts, n - 2) if n < 2 + FT
                            else (h2_parts, n - 2 - FT))
                high, low = (part[:, k, :] for part in parts)
                whole_tile = work[:, n * F:(n + 1) * F]
                nc.gpsimd.tensor_scalar(high, whole_tile, 1.0, None, ALU.mult).then_inc(w_high, 1)
                pool.wait_ge(w_high, n + 1)
                nc.gpsimd.tensor_tensor(low, whole_tile, high, ALU.subtract).then_inc(w_split, 1)

            stretch(0, START["pool"])
            pool.wait_ge(mlp_loaded, 64)
            for n in range(2 + FT):
                split(n)
            with pool.Fori(0, G - 1) as g:
                stretch(g, LOOP["pool"])
            stretch(G - 1, END["pool"])
            rsqrt(2 * NC - 1)
            rsqrt(2 * NC)
            with pool.Fori(0, NC) as c:
                rsqrt(2 * NC + c + 1)

        @block.vector
        def _(dve):
            count, base = [0], [0]

            def link(ins):
                count[0] += 1
                ins.then_inc(vstep, 1)
                dve.wait_ge(vstep, base[0] + count[0])


            def norm_stats(src):
                for j in range(TPC):
                    last = nc.vector.bn_stats(stats[:, j, :], src(j))
                link(last)
                dve.sem_inc(alone, 1)
                for j in range(TPC):
                    last = nc.vector.bn_aggr(mv[:, j, :], stats[:, j, :])
                link(last)
                nc.vector.tensor_scalar(var[:, :], mv[:, :, 1], EPS, None, ALU.add).then_inc(var_ready, 1)

            def normed(dst, src, j):
                return nc.vector.tensor_scalar(dst, src, mv[:, j, 0:1], rstd[:, j:j + 1],
                                               ALU.subtract, ALU.mult)

            nc.vector.memset(QA[P // 2:P, :], 0.0).then_inc(q_padded, 1)
            nc.vector.memset(VA[:, :, :, :, D:VW].rearrange("p g t h v -> p (g t h) v"), 1.0)

            def x_stats_of(c):
                tiles = range(TPC * c, TPC * (c + 1))
                for t in tiles:
                    last = nc.vector.bn_stats(xstats[:, t, :], X[:, t, :])
                link(last)
                for t in tiles:
                    last = nc.vector.bn_aggr(xmv[:, t, :], xstats[:, t, :])
                link(last)
                nc.vector.tensor_scalar(xvar[:, tiles[0]:tiles[-1] + 1], xmv[:, tiles[0]:tiles[-1] + 1, 1], EPS, None,
                                        ALU.add).then_inc(xvar_ready, 1)

            def x_normed(c):
                if not isinstance(c, int):
                    dve.wait_ge(xrstd_ready, c + 1)
                    dve.wait_ge(xn_turned, c + BASE)
                for j in range(TPC):
                    t = bass.ds(TPC * c + j, 1)
                    last = nc.vector.tensor_scalar(XN[:, j, :], X[:, t, :].rearrange("p t f -> p (t f)"),
                                                   xmv[:, t, 0], xrstd[:, t], ALU.subtract, ALU.mult)
                last.then_inc(xn_ready, 1)

            def rotated(c):
                for step in range(TPC + 2):
                    j = step
                    if j < TPC:
                        dve.wait_ge(qkv_ready, TPC * c + j + 1 + BASE)
                        v = VA[:, :, bass.ds(TPC * c + j, 1), :, 0:D].rearrange("p g t h d -> p g (t h) d")
                        nc.vector.tensor_tensor(v, PS[:, j, 2 * C:3 * C].rearrange("p (g h d) -> p g h d", g=G, d=D),
                                                bqkv[:, 2 * C:3 * C].rearrange("p (g h d) -> p g h d", g=G, d=D),
                                                ALU.add)
                        nc.vector.tensor_tensor(qk[:, j, :], PS[:, j, 0:2 * C], bqkv[:, 0:2 * C],
                                                ALU.add).then_inc(qk_ready, 1)
                    j = step - 1
                    if 0 <= j < TPC:
                        dve.wait_ge(qk_ready, TPC * c + j + 1 + BASE)
                        halves = qk[:, j, :].rearrange("p (b h s f) -> p b h s f", b=2, s=2, f=D // 2)
                        turned = rb[:, j, :].rearrange("p (b h s f) -> p b h s f", b=2, s=2, f=D // 2)
                        sin = rope[:, bass.ds(TPC * c + j, 1), 1, :, :].rearrange("p t b f -> p (t b) f")
                        sin = sin.unsqueeze(2).broadcast_to([P, 2, H, D // 2])
                        nc.vector.tensor_tensor(turned[:, :, :, 0, :], halves[:, :, :, 1, :], sin, ALU.mult)
                        nc.vector.tensor_tensor(turned[:, :, :, 1, :], halves[:, :, :, 0, :], sin,
                                                ALU.mult).then_inc(rb_ready, 1)
                    j = step - 2
                    if 0 <= j < TPC:
                        dve.wait_ge(rb_ready, TPC * c + j + 1)
                        dve.wait_ge(ra_ready, TPC * c + j + 1)
                        a, b, r = (t[:, j, :].rearrange("p (n s f) -> p n s f", s=2, f=D // 2) for t in (ra, rb, qr))
                        nc.vector.tensor_tensor(r[:, :, 0, :], a[:, :, 0, :], b[:, :, 0, :], ALU.subtract)
                        nc.vector.tensor_tensor(r[:, :, 1, :], a[:, :, 1, :], b[:, :, 1, :],
                                                ALU.add).then_inc(qr_ready, 1)

            def residues(c):
                dve.wait_ge(lo_ready, TPC * c + BASE)
                for j in range(TPC):
                    dve.wait_ge(hi_ready, TPC * c + j + 1)
                    nc.vector.tensor_tensor(qres[:, j, :], qr[:, j, :], pieces3[:, j, 0, :],
                                            ALU.subtract).then_inc(res_ready, 1)

            dve.wait_ge(x0_loaded, 16)
            x_stats_of(0)
            dve.wait_ge(xrstd_ready, 1)
            x_normed(0)
            dve.wait_ge(x_loaded, 16)
            for c in range(1, NC):
                x_stats_of(c)
            dve.wait_ge(w_loaded, 64)
            nc.vector.tensor_copy(identb[:, :], ident[:, :]).then_inc(idb_ready, 1)
            with dve.Fori(0, NC - 1) as c:
                x_normed(c + 1)
                rotated(c)
                residues(c)
            rotated(NC - 1)
            residues(NC - 1)

            nc.vector.memset(mneg[:, :], 0.0)
            dve.wait_ge(c_loaded, 80)

            def gated(c, m):
                dve.wait_ge(silu_done, FT * c + m + 1)
                if m == 0 and not isinstance(c, int):
                    dve.wait_ge(hB_low, FT * c)
                nc.vector.scalar_tensor_tensor(out=whole[:, m, :], in0=PS[:, 2 * (m % 2) + 1, :],
                                               scalar=scales[:, 1, m:m + 1], in1=silu[:, m % 2, :],
                                               op0=ALU.mult, op1=ALU.mult).then_inc(up_used, 1)

            def stretch(g, items, links):
                base[0], count[0] = links, 0
                for item in items:
                    kind, c = item[0], item[2]
                    grp = g + item[1]
                    if kind == "piece":
                        _, _, _, h, qt, kc = item
                        at = piece_at(c, kc, h, qt)
                        row = h * TPC + qt
                        dve.wait_ge(ps_ready, passed_before(grp, at) + 1)
                        if kc < c:
                            nc.vector.tensor_reduce(mpart[:, row, kc:kc + 1], PS[:, MAXB + at % MAXBANKS, :], AX.X,
                                                    ALU.max).then_inc(ps_used, 1)
                        else:
                            dve.sem_inc(alone, 1)
                            width = (qt + 1) * P
                            nc.vector.tensor_tensor_reduce(junk[:, qt, 0:width], PS[:, MAXB + at % MAXBANKS, 0:width],
                                                           mask[:, CH - width:CH], 1.0, LOWEST, ALU.add, ALU.max,
                                                           mpart[:, row, kc:kc + 1]).then_inc(ps_used, 1)
                    elif kind == "o_clear":
                        dve.wait_ge(pt_copied, NC * TPC + BASE)
                        nc.vector.memset(PS[:, OB, :], 0.0).then_inc(o_clear, 1)
                    elif kind == "neg_split":
                        dve.wait_ge(ps_used, passed_before(grp, piece_at(c, c, HG - 1, TPC - 1)) + 1)
                        hi, mid, lo = (mneg[:, a * HG * TPC:(a + 1) * HG * TPC] for a in range(PARTS))
                        link(nc.vector.tensor_reduce(mx[:, :], mpart[:, :, 0:c + 1], AX.X, ALU.max))
                        link(nc.vector.tensor_scalar(hi, mx[:, :], -1.0, None, ALU.mult))
                        link(nc.vector.scalar_tensor_tensor(out=mres[:, :], in0=mx[:, :], scalar=-1.0, in1=hi,
                                                            op0=ALU.mult, op1=ALU.subtract))
                        link(nc.vector.tensor_copy(mid, mres[:, :]))
                        nc.vector.tensor_tensor(lo, mres[:, :], mid, ALU.subtract).then_inc(neg_ready, 1)
                    elif kind == "neg_copy":
                        at, bank = neg_passage(grp, c)
                        dve.wait_ge(ps_ready, passed_before(grp, at) + 1)
                        dve.wait_ge(negs_loaded[c], 16 * grp + BASE)
                        nc.vector.tensor_copy(mT[0:PARTS * HG * TPC, c, :],
                                              PS[0:PARTS * HG * TPC, MAXB + bank, :].bitcast(bf16)[:, 0:P]
                                              ).then_inc(ps_used, 1)
                    elif kind == "vg":
                        copy_values(grp)
                    elif kind == "o_norm":
                        dve.wait_ge(o_turned, NC * grp + c + 1)
                        o = PS[:, OB, :].rearrange("p (j h v) -> p j h v", j=TPC, h=HG)
                        r = rec[:, :].rearrange("p (j h v) -> p j h v", j=TPC, h=HG)
                        link(nc.vector.reciprocal(r, o[:, :, :, D:VW]))
                        dst = AT[:, TPC * c:TPC * (c + 1), bass.ds(grp * HG * D, HG * D)]
                        nc.vector.tensor_tensor(dst.rearrange("p j (h d) -> p j h d", d=D), o[:, :, :, 0:D],
                                                r.broadcast_to([P, TPC, HG, D]), ALU.mult).then_inc(at_ready, 1)
                    elif kind == "a_copy":
                        a_copy(c, MISC)
                    elif kind == "y_stats":
                        y_stats(c, MISC)
                    elif kind == "x_stats":
                        x_stats(c)
                    elif kind == "x_norm":
                        x_norm(c)
                    elif kind == "x_copy":
                        x2_copy(c, MISC)
                    elif kind == "gated":
                        gated(0, c)

            def a_copy(c, bank):
                dve.wait_ge(a_turned, c + 1)
                nc.vector.tensor_copy(aT[:, :], PS[:, bank, :]).then_inc(aT_ready, 1)

            def y_stats(c, bank):
                dve.wait_ge(proj_ready, c + 1)
                y = PS[:, bank, :].rearrange("p (j f) -> p j f", j=TPC)
                bias = bo[:, :].unsqueeze(1).broadcast_to([P, TPC, C])
                nc.vector.tensor_tensor(yb[:, :, :], y, bias, ALU.add).then_inc(proj_used, 1)
                dve.wait_ge(proj_used, c + 1)
                norm_stats(lambda j: yb[:, j, :])

            def x_stats(c):
                dve.wait_ge(rstd_ready, 2 * c + 1)
                if c > 0:
                    dve.wait_ge(x2n_turned, c)
                for j in range(TPC):
                    last = normed(yn[:, j, :], yb[:, j, :], j)
                link(last)
                xc = X[:, TPC * c:TPC * (c + 1), :]
                link(nc.vector.tensor_tensor(xc, xc, yn[:, :, :], ALU.add))
                norm_stats(lambda j: X[:, TPC * c + j, :])

            def x_norm(c):
                dve.wait_ge(rstd_ready, 2 * c + 2)
                for j in range(TPC):
                    last = normed(yn[:, j, :], X[:, TPC * c + j, :], j)
                last.then_inc(x2n_ready, 1)

            def x2_copy(c, bank):
                dve.wait_ge(x2n_turned, c + 1)
                cols = slice(c * CH, (c + 1) * CH)
                link(nc.vector.tensor_copy(X2T_high[:, cols], PS[:, bank, :]))
                nc.vector.tensor_tensor(X2T_low[:, cols], PS[:, bank, :], X2T_high[:, cols],
                                        ALU.subtract).then_inc(x2t_ready, 1)

            def copy_values(grp):
                if not (isinstance(grp, int) and grp == 0):
                    dve.wait_ge(pv_done, STEPS * grp)
                vg = VA[:, bass.ds(grp, 1), :, :, :].rearrange("p g t h v -> p (g t h v)")
                nc.vector.tensor_copy(VG[:, :, :, :].rearrange("p t h v -> p (t h v)"), vg).then_inc(vg_ready, 1)

            def links_in(items):
                return sum({"neg_split": 4, "o_norm": 1}.get(item[0], 0) for item in items)

            copy_values(0)
            first_links = count[0]
            before, per = first_links + links_in(START["dve"]), links_in(LOOP["dve"])
            stretch(0, START["dve"], first_links)
            with dve.Fori(0, G - 1) as g:
                stretch(g, LOOP["dve"], before + per * g)
            stretch(G - 1, END["dve"], before + per * (G - 1))

            def hA_rest(c, m):
                dve.wait_ge(hA_high, FT * c + m + 1)
                nc.vector.tensor_tensor(hA_parts[1][:, m, :], whole[:, m, :], hA_parts[0][:, m, :],
                                        ALU.subtract).then_inc(hA_low, 1)

            def hB_rest(c):
                for m in range(FT):
                    dve.wait_ge(hB_whole, FT * c + m + 1)
                    nc.vector.tensor_tensor(hB_parts[1][:, m, :], whole[:, m, :], hB_parts[0][:, m, :],
                                            ALU.subtract).then_inc(hB_low, 1)

            def out_scaled(c):
                dve.wait_ge(y_ready, c + 1)
                nc.vector.tensor_tensor(yb[:, :, :], PS[:, 4:8, 0:C],
                                        s3[:, :].unsqueeze(1).broadcast_to([P, TPC, C]),
                                        ALU.mult).then_inc(y_used, 1)

            def out_stats(c):
                dve.wait_ge(y_used, c + 1 + BASE)
                norm_stats(lambda j: yb[:, j, :])

            def out(c):
                dve.wait_ge(rstd_ready, 2 * NC + c + 1)
                for j in range(TPC):
                    last = normed(yn[:, j, :], yb[:, j, :], j)
                link(last)
                dve.wait_ge(o_stored, 16 * c + BASE)
                nc.vector.tensor_tensor(ob[:, :, :], X[:, bass.ds(TPC * c, TPC), :], yn[:, :, :],
                                        ALU.add).then_inc(o_ready, 1)

            x_norm(NC - 2)
            a_copy(NC - 1, OB)
            gated(0, 1)
            x2_copy(NC - 2, MISC)
            y_stats(NC - 1, OB)
            hA_rest(0, 0)
            gated(0, 2)
            hA_rest(0, 1)
            gated(0, 3)
            x_stats(NC - 1)
            hA_rest(0, 2)
            hA_rest(0, 3)
            x_norm(NC - 1)
            x2_copy(NC - 1, 0)
            hB_rest(0)
            out_scaled(0)
            start, LINKS_M = base[0] + count[0], 3
            with dve.Fori(0, NC - 1) as last_c:
                base[0], count[0] = start + LINKS_M * last_c, 0
                c = last_c + 1
                gated(c, 0)
                gated(c, 1)
                out_stats(last_c)
                hA_rest(c, 0)
                gated(c, 2)
                hA_rest(c, 1)
                gated(c, 3)
                hA_rest(c, 2)
                hA_rest(c, 3)
                out(last_c)
                hB_rest(c)
                out_scaled(c)
                assert count[0] == LINKS_M
            base[0], count[0] = start + LINKS_M * (NC - 1), 0
            out_stats(NC - 1)
            out(NC - 1)


def rope_tables():
    inv_freq = (1.0 / np.float32(ROPE_BASE) ** (np.arange(0, D, 2, dtype=np.float32) / D)).astype(np.float32)
    freqs = (np.arange(T, dtype=np.float32)[:, None] * inv_freq[None, :]).astype(np.float64)
    scale = 1.0 / np.sqrt(D)
    tables = np.stack([np.stack([f(freqs) * scale, f(freqs)], 1) for f in (np.cos, np.sin)], 1)
    tables = tables.reshape(T // P, P, 4 * D // 2).transpose(1, 0, 2)
    return np.ascontiguousarray(tables.reshape(P, -1), dtype=np.float32)


def kernel(L0_attn_x, L0_attn_Wq, L0_attn_bq, L0_attn_Wk, L0_attn_bk, L0_attn_Wv, L0_attn_bv, L0_attn_Wo,
           L0_attn_bo, L0_ffn_w1_w, L0_ffn_w1_s, L0_ffn_w2_w, L0_ffn_w2_s, L0_ffn_h1_w, L0_ffn_h1_s,
           L0_ffn_h2_w, L0_ffn_h2_s, L0_ffn_w3_w, L0_ffn_w3_s):
    import ml_dtypes
    import concourse.bacc as bacc
    from concourse.bass_utils import run_bass_kernel_spmd

    def lay(a):
        return np.ascontiguousarray(a)

    def columns(s):
        return np.asarray(s).reshape(FT, P).T

    tri = np.where(np.arange(P)[None, :] > np.arange(P)[:, None], np.float32(LOWEST), np.float32(0))
    arrays = {
        "x": lay(np.asarray(L0_attn_x).reshape(T, C)),
        "wqkv": lay(np.concatenate([np.asarray(w).T for w in (L0_attn_Wq, L0_attn_Wk, L0_attn_Wv)], 1)),
        "bqkv": lay(np.concatenate([np.asarray(b) for b in (L0_attn_bq, L0_attn_bk, L0_attn_bv)])[None, :]),
        "wo": lay(np.asarray(L0_attn_Wo).T),
        "bo": lay(np.asarray(L0_attn_bo)[None, :]),
        "w12": lay(np.concatenate([np.asarray(L0_ffn_w1_w).T, np.asarray(L0_ffn_w2_w).T], 1)),
        "h1": lay(np.asarray(L0_ffn_h1_w).T),
        "h2": lay(np.asarray(L0_ffn_h2_w).T),
        "w3": lay(np.asarray(L0_ffn_w3_w).T),
        "scales": lay(np.concatenate([columns(s) for s in (L0_ffn_w1_s, L0_ffn_w2_s, L0_ffn_h1_s,
                                                           L0_ffn_h2_s)], 1)),
        "s3": lay(np.asarray(L0_ffn_w3_s)[None, :]),
        "ident": np.eye(P, dtype=np.float32),
        "mask": lay(np.concatenate([np.zeros((P, CH - P), np.float32), tri], 1)),
        "rope": rope_tables(),
        "ones": np.ones((PARTS, COLS), ml_dtypes.bfloat16),
    }
    nc = bacc.Bacc("TRN2", target_bir_lowering=False, num_devices=1)
    args = [nc.dram_tensor(f"in_{n}", a.shape, mybir.dt.from_np(a.dtype), kind="ExternalInput").ap()
            for n, a in arrays.items()]
    out = nc.dram_tensor("out_y", (T, C), mybir.dt.float32, kind="ExternalOutput").ap()
    attention_mlp_kernel(nc, *args, out)
    r = run_bass_kernel_spmd(nc, [{f"in_{n}": a for n, a in arrays.items()}], core_ids=[0])
    return r.results[0]["out_y"].reshape(1, T, C)
```
